# Optimizing a Trainium2 kernel written in Bass

```python
import numpy as np
import jax
import jax.numpy as jnp

def _softmax(x, axis=-1):
    return jax.nn.softmax(x, axis=axis)

def _gelu(x):
    return jax.nn.gelu(x, approximate=True)

def _silu(x):
    return jax.nn.silu(x)

def _sigmoid(x):
    return jax.nn.sigmoid(x)

def _layernorm(x, axis=-1, eps=1e-05):
    m = jnp.mean(x, axis=axis, keepdims=True)
    v = jnp.var(x, axis=axis, keepdims=True)
    return (x - m) / jnp.sqrt(v + eps)

def _scatter_add(tgt, idx, src, axis=0):
    return tgt.at[idx].add(src)

def _segment_sum(src, seg, n):
    return jax.ops.segment_sum(src, seg, n)
kernel_name = 'mk_gnn_resnorm_d1_gnn_r8_0dd9b1'

def setup_inputs(seed: int=0):
    np.random.seed(seed)
    _w = jnp.asarray

    def _rec_inputs():
        import jax
        import jax.numpy as jnp
        _gk = jax.random.key(seed)
        x = -0.000202 + 1 * jax.random.normal(jax.random.fold_in(_gk, 1), (12500, 128), jnp.float32)
        _s = jax.random.randint(jax.random.fold_in(_gk, 2), (100000,), 0, 12500, jnp.int32)
        _d = jax.random.randint(jax.random.fold_in(_gk, 3), (100000,), 0, 12500, jnp.int32)
        _loop = jnp.arange(12500, dtype=jnp.int32)
        src = jnp.concatenate([_s, _d, _loop])
        dst = jnp.concatenate([_d, _s, _loop])
        _o = jnp.argsort(dst, stable=True)
        src = src[_o]
        dst = dst[_o]
        edge_attr_128 = -5.16925e-05 + 1.00005 * jax.random.normal(jax.random.fold_in(_gk, 11), (212500, 128), jnp.float32)
        return (x, src, dst, edge_attr_128)
    x, src, dst, edge_attr_128 = _rec_inputs()

    def _L0_gnn_setup():
        import jax, jax.numpy as jnp
        import numpy as np
        N, E, D = (6250, 100000, 128)
        LN_EPS = 1e-05
        key = jax.random.key(seed)
        ks = jax.random.split(key, 8)
        x = jax.random.normal(ks[0], (N, D), dtype=jnp.float32)
        edge_index = jax.random.randint(ks[1], (2, E), 0, N, dtype=jnp.int64)
        edge_attr = jax.random.normal(ks[2], (E, D), dtype=jnp.float32)
        s_msg = 1.0 / np.sqrt(2 * D)
        s_upd = 1.0 / np.sqrt(2 * D)
        W_msg = jax.random.uniform(ks[3], (2 * D, D), jnp.float32, -s_msg, s_msg)
        b_msg = jax.random.uniform(ks[4], (D,), jnp.float32, -s_msg, s_msg)
        W_upd = jax.random.uniform(ks[5], (2 * D, D), jnp.float32, -s_upd, s_upd)
        b_upd = jax.random.uniform(ks[6], (D,), jnp.float32, -s_upd, s_upd)
        gamma = jnp.ones((D,), jnp.float32)
        beta = jnp.zeros((D,), jnp.float32)
        return {'x': x, 'edge_index': edge_index, 'edge_attr': edge_attr, 'W_msg': W_msg, 'b_msg': b_msg, 'W_upd': W_upd, 'b_upd': b_upd, 'gamma': gamma, 'beta': beta}
    _L0_gnn_all = _L0_gnn_setup()
    _L0_gnn_in = {k: v for k, v in _L0_gnn_all.items() if k in ('W_msg', 'b_msg', 'W_upd', 'b_upd', 'gamma', 'beta')}
    del _L0_gnn_all
    return {'x': x, 'src': src, 'dst': dst, 'edge_attr_128': edge_attr_128, 'L0_gnn_W_msg': _L0_gnn_in['W_msg'], 'L0_gnn_b_msg': _L0_gnn_in['b_msg'], 'L0_gnn_W_upd': _L0_gnn_in['W_upd'], 'L0_gnn_b_upd': _L0_gnn_in['b_upd'], 'L0_gnn_gamma': _L0_gnn_in['gamma'], 'L0_gnn_beta': _L0_gnn_in['beta']}

def reference(x, src, dst, edge_attr_128, L0_gnn_W_msg, L0_gnn_b_msg, L0_gnn_W_upd, L0_gnn_b_upd, L0_gnn_gamma, L0_gnn_beta):
    import jax
    import jax.numpy as jnp

    def _L0_gnn_ref(x, edge_index, edge_attr, W_msg, b_msg, W_upd, b_upd, gamma, beta):
        import jax, jax.numpy as jnp
        import numpy as np
        N, E, D = (6250, 100000, 128)
        LN_EPS = 1e-05
        src, dst = (edge_index[0], edge_index[1])
        n = x.shape[0]
        msg_in = jnp.concatenate([x[src], edge_attr], axis=-1)
        msg = jax.nn.relu(msg_in @ W_msg + b_msg)
        summed = jax.ops.segment_sum(msg, dst, num_segments=n)
        counts = jax.ops.segment_sum(jnp.ones((msg.shape[0],), x.dtype), dst, num_segments=n)
        mean_msg = summed / jnp.maximum(counts, 1.0)[:, None]
        h = jnp.concatenate([x, mean_msg], axis=-1) @ W_upd + b_upd
        mu = jnp.mean(h, axis=-1, keepdims=True)
        var = jnp.mean(jnp.square(h - mu), axis=-1, keepdims=True)
        h = (h - mu) * jax.lax.rsqrt(var + LN_EPS) * gamma + beta
        return jax.nn.relu(h + x)
    edge_index = jnp.stack([src, dst])
    x = _layernorm(x + _L0_gnn_ref(x, edge_index, edge_attr_128, L0_gnn_W_msg, L0_gnn_b_msg, L0_gnn_W_upd, L0_gnn_b_upd, L0_gnn_gamma, L0_gnn_beta), axis=-1)
    return x

_drawn_inputs = setup_inputs


def setup_inputs(seed=0):
    import zlib

    import numpy as np

    out = dict(_drawn_inputs(seed))
    spreads = {'L0_gnn_gamma': (1.0, 0.2), 'L0_gnn_beta': (0.0, 0.1)}
    factors = {'L0_gnn_b_msg': 6.934}
    for name, (base, spread) in spreads.items():
        noise = np.random.default_rng([zlib.crc32(name.encode()), seed]).standard_normal(out[name].shape)
        drawn = base * np.exp(spread * noise) if base else spread * noise
        out[name] = jnp.asarray(drawn.astype(out[name].dtype))
    for name, factor in factors.items():
        out[name] = (out[name] * factor).astype(out[name].dtype)
    return out
```

```python
from contextlib import ExitStack

import concourse.bass as bass
from concourse import mybir

P = 128
TILES = 16
GROUP = 4
GROUPS = TILES // GROUP
BLOCK = TILES * P
RING = 2 * GROUPS
LAG = 2
WIDE = 512
YRING = 5
EPS = 1e-5

ALU = mybir.AluOpType
ACT = mybir.ActivationFunctionType
F32 = mybir.dt.float32
I32 = mybir.dt.int32
U32 = mybir.dt.uint32
BF16 = mybir.dt.bfloat16
AX = mybir.AxisListType


def sizes(n_nodes, n_edges):
    blocks = -(-n_edges // (2 * BLOCK)) * 2
    node_tile = min(P, n_nodes // blocks)
    tiles = -(-n_nodes // node_tile)
    per_pass = WIDE * YRING
    columns = -(-(n_nodes + P) // per_pass) * per_pass
    window = -(-(3 * GROUP * P * n_nodes) // (2 * n_edges) // 16) * 16
    return blocks, node_tile, tiles, columns, max(16, min(window, P))


def graph_layer(nc, xT, x_rows, edgesT, src_tiles, dst_tiles, dst_rows, w_msg, b_msg, w_upd, b_upd, gamma, beta,
                out, n_nodes, n_edges):
    NB, NT, NTILES, COLS, WINDOW = sizes(n_nodes, n_edges)
    F = w_msg.shape[1]
    assert F == P and NTILES > NB - LAG
    NS = NB * GROUPS
    NWIDE = COLS // WIDE
    YGROUPS = COLS // WIDE

    y_dram = nc.dram_tensor("y_rows", [COLS, F], F32).ap()
    spans_dram = nc.dram_tensor("spans_of_blocks", [NB, 2 * GROUPS], I32).ap()

    with ExitStack() as ctx:
        def sb(name, shape, dt=F32):
            return ctx.enter_context(nc.sbuf_tensor(name, shape, dt))

        def sem(name):
            return ctx.enter_context(nc.semaphore(name))

        acc = sb("acc", [P, 2, COLS])
        edge_buf = sb("edge_buf", [P, 2, BLOCK])
        rows = sb("rows", [P, RING, GROUP * F])
        msg = sb("msg", [P, GROUPS, GROUP * F])
        onehot = sb("onehot", [P, GROUPS, GROUP, WINDOW])
        src_idx = sb("src_idx", [P, NB + 2, TILES], I32)
        gather_idx = sb("gather_idx", [P, 2, TILES], I32)
        dst_idx = sb("dst_idx", [P, NB, TILES], I32)
        dst_rel = sb("dst_rel", [P, NB, GROUPS, GROUP])
        spans = sb("spans", [P, NB, 2 * GROUPS], I32)
        iota_i = sb("iota_i", [P, WIDE], I32)
        iota_f = sb("iota_f", [P, WIDE])
        wm = sb("wm", [P, 2, F])
        wu = sb("wu", [P, 2, F])
        bias_msg = sb("bias_msg", [P, F])
        bias_upd = sb("bias_upd", [P, F])
        gamma_b = sb("gamma_b", [P, F])
        beta_b = sb("beta_b", [P, F])
        ones = sb("ones", [P, P], BF16)
        least = sb("least", [P, GROUPS])
        most = sb("most", [P, GROUPS])
        done_nodes = sb("done_nodes", [P, 1], I32)
        done_f = sb("done_f", [P, 1])
        late = sb("late", [P, GROUPS])
        wide = sb("wide", [P, GROUPS])
        found = sb("found", [P, 2 * GROUPS], I32)
        violation = sb("violation", [1, 1], I32)
        xT_buf = sb("xT_buf", [P, 2, NT])
        x_buf = sb("x_buf", [P, 2, F])
        meanT = sb("meanT", [P, NT])
        inv = sb("inv", [P, NT])
        hid = sb("hid", [P, F])
        xbeta = sb("xbeta", [P, F])
        stats = sb("stats", [P, 2, 6])
        moments = sb("moments", [P, 2, 2])
        stdev = sb("stdev", [P, 2])
        rstd = sb("rstd", [P, 2])
        eps = sb("eps", [P, 1])
        out_buf = sb("out_buf", [P, 2, F])
        wide_dst = sb("wide_dst", [P, TILES])
        xT_in = edge_buf[:, :, :].rearrange("p a b -> p (a b)")[:, 0:YRING * WIDE].rearrange("p (k n) -> p k n", k=YRING)
        y_out = rows[:, 0:YRING, :]
        dst_f = msg[:, :, :].rearrange("p a b -> p (a b)")[0:NB, 0:BLOCK].rearrange("p (g e) -> p g e", g=GROUPS)
        dst_row = sb("dst_row", [P, BLOCK], I32)
        wide_onehot = dst_row[:, :].bitcast(F32).rearrange("p (k n) -> p k n", k=GROUP)

        banks = ctx.enter_context(nc.psum_tensor("banks", [P, 8, 512], F32))
        zp = banks[:, 0:4, :]
        sums = banks[:, 4:6, :]
        hp = banks[:, 6:8, :]

        consts_in = sem("consts_in")
        idx_in = sem("idx_in")
        dstrow_in = sem("dstrow_in")
        spans_out = sem("spans_out")
        spans_in = sem("spans_in")
        xt_in = [sem(f"xt_in{k}") for k in range(YRING)]
        y_stored = [sem(f"y_stored{k}") for k in range(YRING)]
        y_product = sem("y_product")
        y_ready = sem("y_ready")
        const_made = sem("const_made")
        prep = sem("prep")
        idx_first = sem("idx_first")
        idx_ready = [sem(f"idx_ready{k}") for k in range(2)]
        edges_in = [sem(f"edges_in{k}") for k in range(2)]
        gathered = [sem(f"gathered{k}") for k in range(RING)]
        z_ready = sem("z_ready")
        onehot_ready = sem("onehot_ready")
        added = [sem(f"added{k}") for k in range(RING)]
        relu_done = sem("relu_done")
        sums_ready = sem("sums_ready")
        acc_done = sem("acc_done")
        node_in = [sem(f"node_in{k}") for k in range(2)]
        upd_step = sem("upd_step")
        h_ready = sem("h_ready")
        moments_ready = sem("moments_ready")
        stats_ready = [sem(f"stats_ready{k}") for k in range(4)]
        sqrt_done = sem("sqrt_done")
        out_stored = [sem(f"out_stored{k}") for k in range(2)]
        g_start = sem("g_start")
        g_edges_in = sem("g_edges_in")
        g_idx = sem("g_idx")
        g_gathered = sem("g_gathered")
        g_z = sem("g_z")
        g_added = sem("g_added")
        g_relu = sem("g_relu")
        g_dst = sem("g_dst")
        g_onehot = sem("g_onehot")
        g_used = sem("g_used")
        g_stats = [sem(f"g_stats{k}") for k in range(2)]
        g_acc = sem("g_acc")
        g_node_in = sem("g_node_in")
        g_stored = sem("g_stored")

        block = ctx.enter_context(nc.Block())

        CONSTS = 5
        PREP = 13
        STEPS = 11
        UPDATES = NTILES

        def parity(n):
            return n % 2

        def block_of(i, half):
            return 2 * i + half


        def node_load(sp, t, slot, landed):
            sp.dma_start(xT_buf[:, slot, :], xT[:, bass.ds(t * NT, NT)]).then_inc(landed, 16)
            sp.dma_start(x_buf[0:NT, slot, :], x_rows[bass.ds(t * NT, NT), :]).then_inc(landed, 16)

        def node_store(sp, t, slot, stored):
            sp.dma_start(out[bass.ds(t * NT, NT), :], out_buf[0:NT, slot, :]).then_inc(stored, 16)

        @block.sync
        def _(sp):
            sp.dma_start(dst_row[0:NB, :], dst_rows).then_inc(dstrow_in, 16)
            sp.dma_start(wm[:, :, :], w_msg.rearrange("(a p) n -> p a n", p=P)).then_inc(consts_in, 16)
            sp.dma_start(bias_msg[:, :], b_msg.partition_broadcast(P)).then_inc(consts_in, 16)
            for k in range(YRING):
                sp.dma_start(xT_in[:, k, :], xT[:, k * WIDE:(k + 1) * WIDE]).then_inc(xt_in[k], 16)
            sp.dma_start(dst_idx[:, :, :], dst_tiles).then_inc(idx_in, 16)
            sp.dma_start(src_idx[:, :, :], src_tiles).then_inc(idx_in, 16)
            with sp.Fori(1, YGROUPS // YRING) as i:
                for k in range(YRING):
                    sp.wait_ge(y_product, YRING * i + k - YRING + 1)
                    sp.dma_start(xT_in[:, k, :], xT[:, bass.ds((YRING * i + k) * WIDE, WIDE)]).then_inc(xt_in[k], 16)
            sp.dma_start(wu[:, :, :], w_upd.rearrange("(a p) n -> p a n", p=P)).then_inc(consts_in, 16)
            sp.dma_start(bias_upd[:, :], b_upd.partition_broadcast(P)).then_inc(consts_in, 16)
            sp.dma_start(gamma_b[:, :], gamma.partition_broadcast(P)).then_inc(consts_in, 16)
            sp.dma_start(beta_b[:, :], beta.partition_broadcast(P)).then_inc(consts_in, 16)
            sp.wait_ge(prep, PREP - 3)
            sp.dma_start(spans_dram, found[0:NB, :]).then_inc(spans_out, 16)
            sp.wait_ge(spans_out, 16)
            sp.dma_start(spans[:, :, :], spans_dram.rearrange("(a b) g -> a (b g)", a=1).to_broadcast([P, NB * 2 * GROUPS])).then_inc(spans_in, 16)
            sp.wait_ge(y_product, YGROUPS)

            def fetch(i, half, least):
                b = block_of(i, half)
                if least > 0:
                    sp.wait_ge(z_ready, GROUPS * (b - 2) + GROUPS)
                sp.dma_start(edge_buf[:, half, :], edgesT[b, :, :]).then_inc(edges_in[half], 16)
                if least > 1:
                    sp.wait_ge(upd_step, STEPS * (b - 3))
                    node_store(sp, b - 4, half, out_stored[half])
                if least > 0:
                    node_load(sp, b - 2, half, node_in[half])

            fetch(0, 0, 0)
            fetch(0, 1, 0)
            fetch(1, 0, 1)
            fetch(1, 1, 1)
            with sp.Fori(2, NB // 2) as i:
                fetch(i, 0, 2)
                fetch(i, 1, 2)
            for t in range(NB - LAG, NTILES + LAG):
                slot = parity(t)
                sp.wait_ge(upd_step, STEPS * (t - 1))
                node_store(sp, t - 2, slot, out_stored[slot])
                if t < NTILES:
                    node_load(sp, t, slot, node_in[slot])
            for slot in range(2):
                sp.wait_ge(out_stored[slot], 16 * ((NTILES - slot + 1) // 2))

            broken = sp.value_load(violation[0:1, 0:1], min_val=0, max_val=1)
            with sp.If(broken != 0):
                with sp.Fori(0, NB) as b:
                    sp.wait_ge(g_start, 1)
                    sp.wait_ge(g_z, GROUPS * b)
                    sp.dma_start(edge_buf[:, 0, :], edgesT[b, :, :]).then_inc(g_edges_in, 16)
                with sp.Fori(0, NTILES) as t:
                    node_load(sp, t, 0, g_node_in)
                    sp.wait_ge(upd_step, STEPS * (t + UPDATES + 1))
                    node_store(sp, t, 0, g_stored)
                sp.wait_ge(g_stored, 16 * NTILES)
            with sp.Else():
                sp.nop()

        @block.scalar
        def _(act):
            def store_y(i, k):
                g = YRING * i + k
                act.wait_ge(y_ready, g + 1)
                act.dma_start(y_dram[bass.ds(g * WIDE, WIDE), :].rearrange("(j p) f -> p j f", p=P),
                              y_out[:, k, :].rearrange("p (j f) -> p j f", f=F)).then_inc(y_stored[k], 16)

            with act.Fori(0, YGROUPS // YRING) as i:
                for k in range(YRING):
                    store_y(i, k)

            def square_root(n, which):
                act.wait_ge(moments_ready, 2 * n + which + 1)
                act.activation(stdev[0:NT, which:which + 1], moments[0:NT, which, 1:2], ACT.Sqrt, bias=eps[0:NT, :])\
                   .then_inc(sqrt_done, 1)

            def relu(i, half, peeled):
                for s in range(GROUPS):
                    act.wait_ge(added[GROUPS * half + s], i + 1)
                    act.activation(msg[:, s, :], msg[:, s, :], ACT.Relu).then_inc(relu_done, 1)
                    if s >= 2 and not peeled:
                        square_root(block_of(i, half) - LAG, s - 2)

            act.wait_ge(const_made, CONSTS)
            relu(0, 0, True)
            relu(0, 1, True)
            with act.Fori(1, NB // 2) as i:
                relu(i, 0, False)
                relu(i, 1, False)
            for t in range(NB - LAG, NTILES):
                square_root(t, 0)
                square_root(t, 1)

            act.wait_ge(prep, PREP)
            broken = act.value_load(violation[0:1, 0:1], min_val=0, max_val=1)
            with act.If(broken != 0):
                with act.Fori(0, NB) as b:
                    for s in range(GROUPS):
                        act.wait_ge(g_added, GROUPS * b + s + 1)
                        act.activation(msg[:, s, :], msg[:, s, :], ACT.Relu).then_inc(g_relu, 1)
                with act.Fori(0, NTILES) as t:
                    square_root(t + UPDATES, 0)
                    square_root(t + UPDATES, 1)
            with act.Else():
                act.nop()

        @block.gpsimd
        def _(pool):
            pool.iota(iota_i[:, :], [[1, WIDE]], base=0, channel_multiplier=0).then_inc(const_made, 1)
            pool.iota(done_nodes[:, :], [[0, 1]], base=NT * (1 - LAG), channel_multiplier=NT).then_inc(const_made, 1)
            pool.memset(ones[:, :], 1.0).then_inc(const_made, 1)
            pool.memset(eps[:, :], EPS).then_inc(const_made, 1)
            pool.memset(acc[:, :, :], 0.0).then_inc(const_made, 1)

            def gather(slot, half, tile, done):
                pool.indirect_dma_start(
                    rows[:, slot, tile % GROUP * F:(tile % GROUP + 1) * F], None, y_dram,
                    bass.IndirectOffsetOnAxis(ap=gather_idx[:, half, tile:tile + 1].bitcast(U32), axis=0),
                ).then_inc(done, 16)

            def gather_block(i, half, peeled):
                pool.wait_ge(y_stored[0], 16 * (YGROUPS // YRING))
                if peeled:
                    pool.wait_ge(idx_first, half + 1)
                else:
                    pool.wait_ge(idx_ready[half], i)
                for s in range(GROUPS):
                    slot = GROUPS * half + s
                    if not peeled:
                        pool.wait_ge(y_stored[0], 16 * (YGROUPS // YRING))
                        pool.wait_ge(added[slot], i)
                    for j in range(GROUP):
                        gather(slot, half, GROUP * s + j, gathered[slot])

            for k in range(YRING):
                pool.wait_ge(y_stored[k], 16 * (YGROUPS // YRING))
            gather_block(0, 0, True)
            gather_block(0, 1, True)
            with pool.Fori(1, NB // 2) as i:
                gather_block(i, 0, False)
                gather_block(i, 1, False)

            pool.wait_ge(prep, PREP)
            broken = pool.value_load(violation[0:1, 0:1], min_val=0, max_val=1)
            with pool.If(broken != 0):
                with pool.Fori(1, NB + 1) as n:
                    pool.wait_ge(y_stored[0], 16 * (YGROUPS // YRING))
                    pool.wait_ge(g_idx, n)
                    for s in range(GROUPS):
                        for j in range(GROUP):
                            gather(s, 0, GROUP * s + j, g_gathered)
            with pool.Else():
                pool.nop()

        @block.tensor
        def _(pe):
            pe.wait_ge(consts_in, 32)
            with pe.Fori(0, YGROUPS // YRING) as i:
                for k in range(YRING):
                    g = YRING * i + k
                    pe.wait_ge(xt_in[k], 16 * (i + 1))
                    pe.wait_ge(y_ready, YRING * i)
                    for j in range(GROUP):
                        last = pe.matmul(banks[:, k, j * F:(j + 1) * F], xT_in[:, k, j * P:(j + 1) * P], wm[:, 0, :],
                                         start=True, stop=True)
                    last.then_inc(y_product, 1)
            pe.wait_ge(y_ready, YGROUPS)
            pe.wait_ge(const_made, CONSTS)
            pe.wait_ge(consts_in, 16 * 6)

            def edge_products(s, edges):
                for j in range(GROUP):
                    tile = GROUP * s + j
                    last = pe.matmul(zp[:, s, j * F:(j + 1) * F], edges[:, tile * P:(tile + 1) * P], wm[:, 1, :],
                                     start=True, stop=True)
                return last

            def window_sums(bank_sum, bank_count, s, hot, first=True, final=True):
                for j in range(GROUP):
                    pe.matmul(bank_sum, msg[:, s, j * F:(j + 1) * F], hot[:, j, :],
                              start=(first and j == 0), stop=(final and j == GROUP - 1), skip_group_check=True)
                for j in range(GROUP):
                    last = pe.matmul(bank_count, ones[:, :], hot[:, j, :].bitcast(BF16)[:, 1::2],
                                     start=(first and j == 0), stop=(final and j == GROUP - 1), skip_group_check=True)
                return last

            def sum_group(group, s, peeled):
                bank = s % 2
                pe.wait_ge(relu_done, group + 1)
                pe.wait_ge(onehot_ready, group + 1)
                if not (peeled and group < 2):
                    pe.wait_ge(acc_done, group - 1)
                window_sums(sums[:, bank, 0:WINDOW], sums[:, bank, WINDOW:2 * WINDOW], s, onehot[:, s, :, :])\
                    .then_inc(sums_ready, 1)

            def update(n, t_slot, h_slot, landed, landed_at):
                pe.wait_ge(landed, landed_at)
                pe.matmul(hp[0:NT, h_slot, 0:F], xT_buf[:, t_slot, :], wu[:, 0, :], start=True, stop=False)
                pe.wait_ge(upd_step, STEPS * n + 3)
                pe.matmul(hp[0:NT, h_slot, 0:F], meanT[:, :], wu[:, 1, :], start=False, stop=True).then_inc(h_ready, 1)

            def run_block(i, half, peeled):
                b = block_of(i, half)
                for s in range(GROUPS):
                    group = GROUPS * b + s
                    if s == 0:
                        pe.wait_ge(edges_in[half], 16 * (i + 1))
                    if not (peeled and group < 4):
                        pe.wait_ge(added[GROUPS * (1 - half) + s], i + half)
                    edge_products(s, edge_buf[:, half, :]).then_inc(z_ready, 1)
                    if not (peeled and group < 1):
                        sum_group(group - 1, (s - 1) % GROUPS, peeled)
                    if s == 2 and not peeled:
                        update(b - LAG, half, half, node_in[half], 32 * i)

            run_block(0, 0, True)
            run_block(0, 1, True)
            with pe.Fori(1, NB // 2) as i:
                run_block(i, 0, False)
                run_block(i, 1, False)
            sum_group(NS - 1, GROUPS - 1, False)
            for t in range(NB - LAG, NTILES):
                update(t, parity(t), parity(t), node_in[parity(t)], 32 * (t // 2 + 1))

            broken = pe.value_load(violation[0:1, 0:1], min_val=0, max_val=1)
            with pe.If(broken != 0):
                with pe.Fori(0, NB) as b:
                    pe.wait_ge(g_edges_in, 16 * (b + 1))
                    for s in range(GROUPS):
                        pe.wait_ge(g_added, GROUPS * b)
                        edge_products(s, edge_buf[:, 0, :]).then_inc(g_z, 1)
                    with pe.Fori(0, NWIDE) as w:
                        pe.wait_ge(g_relu, GROUPS * (b + 1))
                        pe.wait_ge(g_acc, b * NWIDE + w)
                        for s in range(GROUPS):
                            pe.wait_ge(g_onehot, (b * NWIDE + w) * GROUPS + s + 1)
                            window_sums(sums[:, 0, :], sums[:, 1, :], s, wide_onehot, first=(s == 0),
                                        final=(s == GROUPS - 1)).then_inc(g_used, 1)
                with pe.Fori(0, NTILES) as t:
                    update(t + UPDATES, 0, 0, g_node_in, 32 * (t + 1))
            with pe.Else():
                pe.nop()

        @block.vector
        def _(dve):
            step = [0]

            def prepared(ins):
                step[0] += 1
                ins.then_inc(prep, 1)
                dve.wait_ge(prep, step[0])

            dve.wait_ge(const_made, 3)
            prepared(dve.tensor_copy(iota_f[:, :], iota_i[:, :]))
            prepared(dve.tensor_copy(done_f[:, :], done_nodes[:, :]))

            def bias_y(i, k, peeled):
                dve.wait_ge(y_product, YRING * i + k + 1)
                if not peeled:
                    dve.wait_ge(y_stored[k], 16 * i)
                dve.tensor_tensor(y_out[:, k, :].rearrange("p (j f) -> p j f", f=F),
                                  banks[:, k, :].rearrange("p (j f) -> p j f", f=F),
                                  bias_msg[:, :].unsqueeze(1).to_broadcast([P, GROUP, F]), ALU.add).then_inc(y_ready, 1)

            for k in range(YRING):
                if k == 0:
                    dve.wait_ge(consts_in, 32)
                bias_y(0, k, True)
            with dve.Fori(1, YGROUPS // YRING) as i:
                for k in range(YRING):
                    bias_y(i, k, False)

            dve.wait_ge(idx_in, 32)
            for half in range(2):
                dve.tensor_copy(gather_idx[:, half, :], src_idx[:, half, :]).then_inc(idx_first, 1)

            dve.wait_ge(dstrow_in, 16)
            prepared(dve.tensor_copy(dst_f, dst_row[0:NB, :].rearrange("p (g e) -> p g e", g=GROUPS)))
            prepared(dve.tensor_reduce(least[0:NB, :], dst_f, AX.X, ALU.min))
            prepared(dve.tensor_reduce(most[0:NB, :], dst_f, AX.X, ALU.max))
            prepared(dve.tensor_scalar(late[0:NB, :], least[0:NB, :], -1.0, done_f[0:NB, 0:1], ALU.mult, ALU.add))
            prepared(dve.tensor_tensor(wide[0:NB, :], most[0:NB, :], least[0:NB, :], ALU.subtract))
            prepared(dve.scalar_tensor_tensor(wide[0:NB, :], wide[0:NB, :], float(1 - WINDOW), late[0:NB, :], ALU.add, ALU.max))
            prepared(dve.tensor_copy(found[0:NB, 0:GROUPS], least[0:NB, :]))
            prepared(dve.tensor_scalar(found[0:NB, GROUPS:2 * GROUPS], wide[0:NB, :], 0.0, None, ALU.is_gt))
            assert step[0] == PREP - 3
            dve.wait_ge(spans_in, 16)
            prepared(dve.tensor_tensor(dst_rel[:, :, :, :],
                                       dst_idx[:, :, :].rearrange("p b (g j) -> p b g j", g=GROUPS),
                                       spans[:, :, 0:GROUPS].unsqueeze(3).to_broadcast([P, NB, GROUPS, GROUP]),
                                       ALU.subtract))
            prepared(dve.tensor_reduce(violation[0:1, 0:1], spans[0:1, :, GROUPS:2 * GROUPS], AX.XY, ALU.max))
            prepared(dve.memset(stats[:, :, :], 0.0))
            assert step[0] == PREP
            dve.wait_ge(const_made, CONSTS)

            def make_onehot(i, half, s, peeled):
                b = block_of(i, half)
                if not (peeled and half == 0):
                    dve.wait_ge(sums_ready, GROUPS * (b - 1) + s + 1)
                dve.tensor_tensor(onehot[:, s, :, :],
                                  iota_f[:, 0:WINDOW].unsqueeze(1).to_broadcast([P, GROUP, WINDOW]),
                                  dst_rel[:, b, s, :].unsqueeze(2).to_broadcast([P, GROUP, WINDOW]),
                                  ALU.is_equal).then_inc(onehot_ready, 1)

            def accumulate(group, s, base, peeled):
                dve.wait_ge(sums_ready, group + 1)
                if not (peeled and group == 0):
                    dve.wait_ge(acc_done, group)
                dve.tensor_tensor(acc[:, :, bass.ds(base, WINDOW)], acc[:, :, bass.ds(base, WINDOW)],
                                  sums[:, s % 2, 0:2 * WINDOW].rearrange("p (a w) -> p a w", a=2),
                                  ALU.add).then_inc(acc_done, 1)

            def base_of(b, s):
                return dve.value_load(spans[0:1, b, s:s + 1], min_val=0, max_val=n_nodes)

            def update_steps(n, t, slot, h_slot, stats_sems, stats_at):
                at = [0]

                def wait():
                    dve.wait_ge(upd_step, STEPS * n + at[0])

                def did(ins):
                    ins.then_inc(upd_step, 1)
                    at[0] += 1

                h = hp[0:NT, h_slot, 0:F]
                x_t = x_buf[0:NT, slot, :]
                r = hid[0:NT, :]
                count = acc[:, 1, bass.ds(t * NT, NT)]
                total = acc[:, 0, bass.ds(t * NT, NT)]

                def moments_of(which, source):
                    wait()
                    dve.bn_stats(stats[0:NT, which, :], source).then_inc(stats_sems[which], 1)
                    dve.wait_ge(const_made, CONSTS)
                    dve.wait_ge(stats_sems[which], stats_at)
                    dve.bn_aggr(moments[0:NT, which, :], stats[0:NT, which, :]).then_inc(moments_ready, 1)

                def invert(which):
                    dve.wait_ge(sqrt_done, 2 * n + which + 1)
                    did(dve.reciprocal(rstd[0:NT, which:which + 1], stdev[0:NT, which:which + 1]))

                def first():
                    did(dve.tensor_scalar(inv[:, :], count, 1.0, None, ALU.max))
                    wait()
                    did(dve.reciprocal(inv[:, :], inv[:, :]))
                    wait()
                    did(dve.tensor_tensor(meanT[:, :], total, inv[:, :], ALU.mult))

                def second():
                    dve.wait_ge(h_ready, n + 1)
                    did(dve.tensor_tensor(r, h, bias_upd[0:NT, :], ALU.add))
                    did(dve.tensor_tensor(xbeta[0:NT, :], x_t, beta_b[0:NT, :], ALU.add))
                    moments_of(0, r)

                def third():
                    invert(0)
                    did(dve.scalar_tensor_tensor(r, r, moments[0:NT, 0, 0:1], gamma_b[0:NT, :], ALU.subtract, ALU.mult))
                    wait()
                    did(dve.scalar_tensor_tensor(r, r, rstd[0:NT, 0:1], xbeta[0:NT, :], ALU.mult, ALU.add))
                    wait()
                    did(dve.scalar_tensor_tensor(r, r, 0.0, x_t, ALU.max, ALU.add))
                    moments_of(1, r)

                def fourth(stored, stored_at):
                    invert(1)
                    wait()
                    dve.wait_ge(stored, stored_at)
                    did(dve.tensor_scalar(out_buf[0:NT, slot, :], r, moments[0:NT, 1, 0:1], rstd[0:NT, 1:2],
                                          ALU.subtract, ALU.mult))
                    assert at[0] == STEPS, at[0]

                return first, second, third, fourth

            def run_block(i, half, peeled):
                b = block_of(i, half)
                if not peeled:
                    first, second, third, fourth = update_steps(b - LAG, b - LAG, half, half, stats_ready[2 * half:2 * half + 2], i)
                for s in range(GROUPS):
                    group = GROUPS * b + s
                    slot = GROUPS * half + s
                    make_onehot(i, half, s, peeled)
                    if s == 1 and not peeled:
                        dve.wait_ge(acc_done, GROUPS * b)
                        first()
                    dve.wait_ge(z_ready, group + 1)
                    dve.wait_ge(gathered[slot], 16 * GROUP * (i + 1))
                    dve.tensor_tensor(msg[:, s, :], zp[:, s, :], rows[:, slot, :], ALU.add).then_inc(added[slot], 1)
                    if s == 1 and not peeled:
                        dve.wait_ge(upd_step, STEPS * (b - LAG) + 3)
                    if not (peeled and group == 0):
                        accumulate(group - 1, (s - 1) % GROUPS, base_of(b, s - 1) if s else base_of(b - 1, GROUPS - 1), peeled)
                    if s == 2 and not peeled:
                        second()
                    if s == 3 and not peeled:
                        third()
                        fourth(out_stored[half], 16 * (i - 1))
                dve.tensor_copy(gather_idx[:, half, :], src_idx[:, b + 2, :]).then_inc(idx_ready[half], 1)

            run_block(0, 0, True)
            run_block(0, 1, True)
            with dve.Fori(1, NB // 2) as i:
                run_block(i, 0, False)
                run_block(i, 1, False)
            accumulate(NS - 1, (NS - 1) % GROUPS, base_of(NB - 1, GROUPS - 1), False)
            dve.wait_ge(acc_done, NS)
            for t in range(NB - LAG, NTILES):
                first, second, third, fourth = update_steps(t, t, parity(t), parity(t),
                                                            stats_ready[2 * parity(t):2 * parity(t) + 2], t // 2 + 1)
                first()
                second()
                third()
                fourth(out_stored[parity(t)], 16 * (t // 2))

            broken = dve.value_load(violation[0:1, 0:1], min_val=0, max_val=1)
            with dve.If(broken != 0):
                dve.wait_ge(upd_step, STEPS * UPDATES)
                dve.memset(acc[:, :, :], 0.0).then_inc(g_start, 1)
                dve.wait_ge(g_start, 1)
                with dve.Fori(0, NB) as b:
                    dve.tensor_copy(gather_idx[:, 0, :], src_idx[:, b, :]).then_inc(g_idx, 1)
                    for s in range(GROUPS):
                        dve.wait_ge(g_z, GROUPS * b + s + 1)
                        dve.wait_ge(g_gathered, 16 * TILES * (b + 1))
                        dve.wait_ge(g_used, NWIDE * GROUPS * b)
                        dve.tensor_tensor(msg[:, s, :], zp[:, s, :], rows[:, s, :], ALU.add).then_inc(g_added, 1)
                    dve.tensor_copy(wide_dst[:, :], dst_idx[:, b, :]).then_inc(g_dst, 1)
                    with dve.Fori(0, NWIDE) as w:
                        dve.wait_ge(g_dst, b * (NWIDE + 1) + w + 1)
                        for s in range(GROUPS):
                            dve.wait_ge(g_used, (b * NWIDE + w) * GROUPS + s)
                            dve.tensor_tensor(wide_onehot,
                                              iota_f[:, :].unsqueeze(1).to_broadcast([P, GROUP, WIDE]),
                                              wide_dst[:, GROUP * s:GROUP * (s + 1)].unsqueeze(2)
                                              .to_broadcast([P, GROUP, WIDE]), ALU.is_equal).then_inc(g_onehot, 1)
                        dve.wait_ge(g_onehot, (b * NWIDE + w) * GROUPS + GROUPS)
                        dve.tensor_scalar(wide_dst[:, :], wide_dst[:, :], float(WIDE), None, ALU.subtract)\
                            .then_inc(g_dst, 1)
                        dve.wait_ge(g_used, (b * NWIDE + w) * GROUPS + GROUPS)
                        dve.wait_ge(g_acc, b * NWIDE + w)
                        dve.tensor_tensor(acc[:, :, bass.ds(w * WIDE, WIDE)], acc[:, :, bass.ds(w * WIDE, WIDE)],
                                          sums[:, :, :], ALU.add).then_inc(g_acc, 1)
                dve.wait_ge(g_acc, NB * NWIDE)
                with dve.Fori(1, NTILES + 1) as m:
                    t = m - 1
                    dve.wait_ge(g_node_in, 32 * m)
                    first, second, third, fourth = update_steps(t + UPDATES, t, 0, 0, g_stats, m)
                    first()
                    second()
                    third()
                    fourth(g_stored, 16 * t)
            with dve.Else():
                dve.nop()


def kernel(x, src, dst, edge_attr_128, L0_gnn_W_msg, L0_gnn_b_msg, L0_gnn_W_upd, L0_gnn_b_upd, L0_gnn_gamma,
           L0_gnn_beta):
    import numpy as np
    import concourse.bacc as bacc
    from concourse.bass_utils import run_bass_kernel_spmd

    x, src, dst, edges = (np.asarray(a) for a in (x, src, dst, edge_attr_128))
    n, f = x.shape
    e = src.shape[0]
    NB, NT, NTILES, COLS, _ = sizes(n, e)

    xT = np.zeros((f, COLS), x.dtype)
    xT[:, :n] = x.T
    x_rows = np.zeros((NTILES * NT, f), x.dtype)
    x_rows[:n] = x
    edges_p = np.zeros((NB * BLOCK, f), edges.dtype)
    edges_p[:e] = edges
    src_p = np.zeros(((NB + 2) * BLOCK,), src.dtype)
    src_p[:e] = src
    dst_p = np.full((NB * BLOCK,), n, dst.dtype)
    dst_p[:e] = dst
    arrays = {
        "xT": xT,
        "x_rows": x_rows,
        "edgesT": np.ascontiguousarray(edges_p.reshape(NB, BLOCK, f).transpose(0, 2, 1)),
        "src_tiles": np.ascontiguousarray(src_p.reshape(NB + 2, TILES, P).transpose(2, 0, 1)),
        "dst_tiles": np.ascontiguousarray(dst_p.reshape(NB, TILES, P).transpose(2, 0, 1)),
        "dst_rows": dst_p.reshape(NB, BLOCK),
        "w_msg": np.asarray(L0_gnn_W_msg),
        "b_msg": np.asarray(L0_gnn_b_msg),
        "w_upd": np.asarray(L0_gnn_W_upd),
        "b_upd": np.asarray(L0_gnn_b_upd),
        "gamma": np.asarray(L0_gnn_gamma),
        "beta": np.asarray(L0_gnn_beta),
    }
    nc = bacc.Bacc("TRN2", target_bir_lowering=False, num_devices=1)
    args = [nc.dram_tensor(name, a.shape, mybir.dt.from_np(a.dtype), kind="ExternalInput").ap()
            for name, a in arrays.items()]
    out = nc.dram_tensor("out", (NTILES * NT, f), mybir.dt.float32, kind="ExternalOutput").ap()
    graph_layer(nc, *args, out, n, e)
    r = run_bass_kernel_spmd(nc, [arrays], core_ids=[0])
    return r.results[0]["out"][:n]
```

```python
from contextlib import ExitStack

import concourse.bass as bass
from concourse import mybir

P = 128
TILES = 16
GROUP = 4
GROUPS = TILES // GROUP
BLOCK = TILES * P
RING = 2 * GROUPS
LAG = 2
WIDE = 512
YRING = 5
EARLY = RING
EPS = 1e-5

ALU = mybir.AluOpType
ACT = mybir.ActivationFunctionType
F32 = mybir.dt.float32
I32 = mybir.dt.int32
U32 = mybir.dt.uint32
BF16 = mybir.dt.bfloat16
AX = mybir.AxisListType


def sizes(n_nodes, n_edges):
    blocks = -(-n_edges // (2 * BLOCK)) * 2
    node_tile = min(P, n_nodes // blocks)
    tiles = -(-n_nodes // node_tile)
    per_pass = WIDE * YRING
    columns = -(-(n_nodes + P) // per_pass) * per_pass
    window = -(-(3 * GROUP * P * n_nodes) // (2 * n_edges) // 16) * 16
    return blocks, node_tile, tiles, columns, max(16, min(window, P))


def graph_layer(nc, xT, x_rows, edgesT, src_tiles, dst_tiles, dst_rows, w_msg, b_msg, w_upd, b_upd, gamma, beta,
                out, n_nodes, n_edges):
    NB, NT, NTILES, COLS, WINDOW = sizes(n_nodes, n_edges)
    F = w_msg.shape[1]
    REST = NTILES - (NB - LAG)
    assert F == P and 0 < REST and REST * F <= 512 and COLS > 2 * YRING * WIDE
    NS = NB * GROUPS
    NWIDE = COLS // WIDE
    YGROUPS = COLS // WIDE

    y_dram = nc.dram_tensor("y_rows", [COLS, F], F32).ap()
    spans_dram = nc.dram_tensor("spans_of_blocks", [NB, 2 * GROUPS], I32).ap()

    with ExitStack() as ctx:
        def sb(name, shape, dt=F32):
            return ctx.enter_context(nc.sbuf_tensor(name, shape, dt))

        def sem(name):
            return ctx.enter_context(nc.semaphore(name))

        acc = sb("acc", [P, 2, COLS])
        edge_buf = sb("edge_buf", [P, 2, BLOCK])
        rows = sb("rows", [P, RING, GROUP * F])
        msg = sb("msg", [P, GROUPS, GROUP * F])
        onehot = sb("onehot", [P, GROUPS, GROUP, WINDOW])
        src_idx = sb("src_idx", [P, NB + 2, TILES], I32)
        gather_idx = sb("gather_idx", [P, 2, TILES], I32)
        dst_idx = sb("dst_idx", [P, NB, TILES], I32)
        dst_rel = sb("dst_rel", [P, NB, GROUPS, GROUP])
        spans = sb("spans", [P, NB, 2 * GROUPS], I32)
        iota_i = sb("iota_i", [P, WIDE], I32)
        iota_f = sb("iota_f", [P, WIDE])
        wm = sb("wm", [P, 2, F])
        wu = sb("wu", [P, 2, F])
        bias_msg = sb("bias_msg", [P, F])
        bias_upd = sb("bias_upd", [P, F])
        gamma_b = sb("gamma_b", [P, F])
        beta_b = sb("beta_b", [P, F])
        ones = sb("ones", [P, P], BF16)
        least = sb("least", [P, GROUPS])
        most = sb("most", [P, GROUPS])
        done_nodes = sb("done_nodes", [P, 1], I32)
        done_f = sb("done_f", [P, 1])
        late = sb("late", [P, GROUPS])
        wide = sb("wide", [P, GROUPS])
        found = sb("found", [P, 2 * GROUPS], I32)
        violation = sb("violation", [1, 1], I32)
        xT_buf = sb("xT_buf", [P, 2, NT])
        x_buf = sb("x_buf", [P, 2, 1, F])
        meanT = sb("meanT", [P, NT])
        inv = sb("inv", [P, NT])
        hid = sb("hid", [P, 1, F])
        xbeta = sb("xbeta", [P, 1, F])
        out_buf = sb("out_buf", [P, 2, 1, F])
        stats = sb("stats", [P, 2, REST, 6])
        moments = sb("moments", [P, 2, REST, 2])
        stdev = sb("stdev", [P, 2, REST])
        rstd = sb("rstd", [P, 2, REST])
        eps = sb("eps", [P, 1])
        zeros = sb("zeros", [P, 1])
        ident = sb("ident", [P, P])
        wide_dst = sb("wide_dst", [P, TILES])
        dst_row = sb("dst_row", [P, BLOCK], I32)
        STAGED = YRING * WIDE
        xT_in = acc[:, 1, COLS - 2 * STAGED:COLS - STAGED].rearrange("p (k n) -> p k n", k=YRING)
        y_out = acc[:, 1, COLS - STAGED:COLS].rearrange("p (k n) -> p k n", k=YRING)
        dst_f = msg[:, :, :].rearrange("p a b -> p (a b)")[0:NB, 0:BLOCK].rearrange("p (g e) -> p g e", g=GROUPS)
        wide_onehot = dst_row[:, :].bitcast(F32).rearrange("p (k n) -> p k n", k=GROUP)
        last = dst_row[:, :].bitcast(F32)
        RF, RN = REST * F, REST * NT
        x_last, xbeta_last, hid_last = (last[:, k * RF:(k + 1) * RF].rearrange("p (t f) -> p t f", f=F) for k in range(3))
        xT_last, inv_last = (last[:, 3 * RF + k * RN:3 * RF + (k + 1) * RN] for k in range(2))
        ident_i = x_buf[:, 0, 0, :].bitcast(I32)
        mean_last = iota_i[:, :].bitcast(F32)[:, 0:RN]

        banks = ctx.enter_context(nc.psum_tensor("banks", [P, 8, 512], F32))
        zp = banks[:, 0:4, :]
        sums = banks[:, 4:6, :]
        hp = banks[:, 6:8, :]

        wm_in = sem("wm_in")
        bias_in = sem("bias_in")
        consts_in = sem("consts_in")
        first_in = sem("first_in")
        idx_in = sem("idx_in")
        dstrow_in = sem("dstrow_in")
        spans_out = sem("spans_out")
        spans_in = sem("spans_in")
        xt_in = [sem(f"xt_in{k}") for k in range(YRING)]
        y_stored = [sem(f"y_stored{k}") for k in range(YRING)]
        y_product = sem("y_product")
        y_ready = sem("y_ready")
        const_made = sem("const_made")
        prep = sem("prep")
        acc_zeroed = sem("acc_zeroed")
        turned = sem("turned")
        turned_back = sem("turned_back")
        idx_ready = [sem(f"idx_ready{k}") for k in range(2)]
        edges_in = [sem(f"edges_in{k}") for k in range(2)]
        gathered = [sem(f"gathered{k}") for k in range(RING)]
        z_ready = sem("z_ready")
        onehot_ready = sem("onehot_ready")
        added = [sem(f"added{k}") for k in range(RING)]
        relu_done = sem("relu_done")
        sums_ready = sem("sums_ready")
        acc_done = sem("acc_done")
        node_in = [sem(f"node_in{k}") for k in range(2)]
        last_in = sem("last_in")
        last_stats = [sem(f"last_stats{k}") for k in range(2)]
        last_stored = sem("last_stored")
        upd_step = sem("upd_step")
        ident_made = sem("ident_made")
        h_ready = sem("h_ready")
        moments_ready = sem("moments_ready")
        stats_ready = [sem(f"stats_ready{k}") for k in range(4)]
        sqrt_done = sem("sqrt_done")
        out_stored = [sem(f"out_stored{k}") for k in range(2)]
        g_start = sem("g_start")
        g_edges_in = sem("g_edges_in")
        g_idx = sem("g_idx")
        g_gathered = sem("g_gathered")
        g_z = sem("g_z")
        g_added = sem("g_added")
        g_relu = sem("g_relu")
        g_dst = sem("g_dst")
        g_onehot = sem("g_onehot")
        g_used = sem("g_used")
        g_stats = [sem(f"g_stats{k}") for k in range(2)]
        g_acc = sem("g_acc")
        g_node_in = sem("g_node_in")
        g_stored = sem("g_stored")

        block = ctx.enter_context(nc.Block())

        CONSTS = 6
        PREP = 13
        STEPS = 11
        UPDATES = NB - LAG + 1

        def parity(n):
            return n % 2

        def block_of(i, half):
            return 2 * i + half


        def node_load(sp, t, slot, landed):
            sp.dma_start(xT_buf[:, slot, :], xT[:, bass.ds(t * NT, NT)]).then_inc(landed, 16)
            sp.dma_start(x_buf[0:NT, slot, 0, :], x_rows[bass.ds(t * NT, NT), :]).then_inc(landed, 16)

        def node_store(sp, t, slot, stored):
            sp.dma_start(out[bass.ds(t * NT, NT), :], out_buf[0:NT, slot, 0, :]).then_inc(stored, 16)

        @block.sync
        def _(sp):
            sp.dma_start(wm[:, :, :], w_msg.rearrange("(a p) n -> p a n", p=P)).then_inc(wm_in, 16)
            for k in range(YRING):
                sp.dma_start(xT_in[:, k, :], xT[:, k * WIDE:(k + 1) * WIDE]).then_inc(xt_in[k], 16)

            def store_y(i, k):
                g = YRING * i + k
                sp.wait_ge(y_ready, g + 1)
                sp.dma_start(y_dram[bass.ds(g * WIDE, WIDE), :].rearrange("(j p) f -> p j f", p=P),
                             y_out[:, k, :].rearrange("p (j f) -> p j f", f=F)).then_inc(y_stored[k], 16)

            with sp.Fori(1, YGROUPS // YRING) as i:
                for k in range(YRING):
                    sp.wait_ge(y_product, YRING * i + k - YRING + 1)
                    sp.dma_start(xT_in[:, k, :], xT[:, bass.ds((YRING * i + k) * WIDE, WIDE)]).then_inc(xt_in[k], 16)
                    store_y(i - 1, k)
            for half in range(2):
                sp.dma_start(edge_buf[:, half, :], edgesT[half, :, :]).then_inc(edges_in[half], 16)
            for k in range(YRING):
                store_y(YGROUPS // YRING - 1, k)

            def fetch(i, half, least):
                b = block_of(i, half)
                sp.wait_ge(z_ready, GROUPS * (b - 2) + GROUPS)
                sp.dma_start(edge_buf[:, half, :], edgesT[b, :, :]).then_inc(edges_in[half], 16)
                if least > 1:
                    sp.wait_ge(upd_step, STEPS * (b - 3))
                    node_store(sp, b - 4, half, out_stored[half])
                node_load(sp, b - 2, half, node_in[half])

            fetch(1, 0, 1)
            fetch(1, 1, 1)
            with sp.Fori(2, NB // 2) as i:
                fetch(i, 0, 2)
                fetch(i, 1, 2)
            t0 = NB - LAG
            sp.dma_start(xT_last, xT[:, t0 * NT:NTILES * NT]).then_inc(last_in, 16)
            sp.dma_start(x_last[0:NT, :, :], x_rows[t0 * NT:NTILES * NT, :].rearrange("(t p) f -> p t f", p=NT))\
              .then_inc(last_in, 16)
            for t in (t0 - 2, t0 - 1):
                sp.wait_ge(upd_step, STEPS * (t + 1))
                node_store(sp, t, parity(t), out_stored[parity(t)])
            sp.wait_ge(upd_step, STEPS * UPDATES)
            sp.dma_start(out[t0 * NT:NTILES * NT, :].rearrange("(t p) f -> p t f", p=NT), hid_last[0:NT, :, :])\
              .then_inc(last_stored, 16)
            for slot in range(2):
                sp.wait_ge(out_stored[slot], 16 * (t0 // 2))
            sp.wait_ge(last_stored, 16)

            broken = sp.value_load(violation[0:1, 0:1], min_val=0, max_val=1)
            with sp.If(broken != 0):
                with sp.Fori(0, NB) as b:
                    sp.wait_ge(g_start, 1)
                    sp.wait_ge(g_z, GROUPS * b)
                    sp.dma_start(edge_buf[:, 0, :], edgesT[b, :, :]).then_inc(g_edges_in, 16)
                with sp.Fori(0, NTILES) as t:
                    node_load(sp, t, 0, g_node_in)
                    sp.wait_ge(upd_step, STEPS * (t + UPDATES + 1))
                    node_store(sp, t, 0, g_stored)
                sp.wait_ge(g_stored, 16 * NTILES)
            with sp.Else():
                sp.nop()

        @block.scalar
        def _(act):
            act.dma_start(gather_idx[:, :, :], src_tiles[:, 0:2, :]).then_inc(first_in, 16)
            act.dma_start(dst_row[0:NB, :], dst_rows).then_inc(dstrow_in, 16)
            act.dma_start(bias_msg[:, :], b_msg.partition_broadcast(P)).then_inc(bias_in, 16)
            act.dma_start(dst_idx[:, :, :], dst_tiles).then_inc(idx_in, 16)
            act.dma_start(src_idx[:, :, :], src_tiles).then_inc(idx_in, 16)
            act.dma_start(wu[:, :, :], w_upd.rearrange("(a p) n -> p a n", p=P)).then_inc(consts_in, 16)
            act.dma_start(bias_upd[:, :], b_upd.partition_broadcast(P)).then_inc(consts_in, 16)
            act.dma_start(gamma_b[:, :], gamma.partition_broadcast(P)).then_inc(consts_in, 16)
            act.dma_start(beta_b[:, :], beta.partition_broadcast(P)).then_inc(consts_in, 16)

            def zero(columns):
                act.activation(columns, zeros[:, :].to_broadcast([P, columns.shape[1]]), ACT.Copy).then_inc(acc_zeroed, 1)

            act.wait_ge(const_made, CONSTS)
            zero(acc[:, 0, :])
            act.wait_ge(prep, PREP - 3)
            act.dma_start(spans_dram, found[0:NB, :]).then_inc(spans_out, 16)
            act.wait_ge(spans_out, 16)
            act.dma_start(spans[:, :, :].rearrange("p b g -> p (b g)"),
                          spans_dram.rearrange("(a b) g -> a (b g)", a=1).to_broadcast([P, NB * 2 * GROUPS]))\
               .then_inc(spans_in, 16)
            zero(acc[:, 1, 0:COLS - 2 * STAGED])
            for group in range(EARLY):
                act.wait_ge(turned, group + 1)
                act.activation(rows[:, group, :], banks[:, 6 + group % 2, :], ACT.Copy).then_inc(turned_back, 1)
            act.wait_ge(y_product, YGROUPS)
            for k in range(YRING):
                act.wait_ge(y_stored[k], 16 * (YGROUPS // YRING))
            zero(acc[:, 1, COLS - 2 * STAGED:COLS])

            def square_root(n, which, tiles=1):
                act.wait_ge(moments_ready, 2 * n + which + 1)
                act.activation(stdev[0:NT, which, 0:tiles], moments[0:NT, which, 0:tiles, 1], ACT.Sqrt, bias=eps[0:NT, :])\
                   .then_inc(sqrt_done, 1)

            def relu(i, half, peeled):
                for s in range(GROUPS):
                    act.wait_ge(added[GROUPS * half + s], i + 1)
                    act.activation(msg[:, s, :], msg[:, s, :], ACT.Relu).then_inc(relu_done, 1)
                    if s >= 2 and not peeled:
                        square_root(block_of(i, half) - LAG, s - 2)

            relu(0, 0, True)
            relu(0, 1, True)
            with act.Fori(1, NB // 2) as i:
                relu(i, 0, False)
                relu(i, 1, False)
            square_root(UPDATES - 1, 0, REST)
            square_root(UPDATES - 1, 1, REST)

            act.wait_ge(prep, PREP)
            broken = act.value_load(violation[0:1, 0:1], min_val=0, max_val=1)
            with act.If(broken != 0):
                with act.Fori(0, NB) as b:
                    for s in range(GROUPS):
                        act.wait_ge(g_added, GROUPS * b + s + 1)
                        act.activation(msg[:, s, :], msg[:, s, :], ACT.Relu).then_inc(g_relu, 1)
                with act.Fori(0, NTILES) as t:
                    square_root(t + UPDATES, 0)
                    square_root(t + UPDATES, 1)
            with act.Else():
                act.nop()

        @block.gpsimd
        def _(pool):
            pool.iota(iota_i[:, :], [[1, WIDE]], base=0, channel_multiplier=0).then_inc(const_made, 1)
            pool.iota(done_nodes[:, :], [[0, 1]], base=NT * (1 - LAG), channel_multiplier=NT).then_inc(const_made, 1)
            pool.memset(ones[:, :], 1.0).then_inc(const_made, 1)
            pool.memset(eps[:, :], EPS).then_inc(const_made, 1)
            pool.memset(zeros[:, :], 0.0).then_inc(const_made, 1)
            pool.iota(ident_i, [[1, P]], base=0, channel_multiplier=-1).then_inc(const_made, 1)

            def gather(table, slot, half, tile, done):
                pool.indirect_dma_start(
                    rows[:, slot, tile % GROUP * F:(tile % GROUP + 1) * F], None, table,
                    bass.IndirectOffsetOnAxis(ap=gather_idx[:, half, tile:tile + 1].bitcast(U32), axis=0),
                ).then_inc(done, 16)

            def gather_block(i, half):
                pool.wait_ge(y_stored[0], 16 * (YGROUPS // YRING))
                pool.wait_ge(idx_ready[half], i)
                for s in range(GROUPS):
                    slot = GROUPS * half + s
                    pool.wait_ge(y_stored[0], 16 * (YGROUPS // YRING))
                    pool.wait_ge(added[slot], i)
                    for j in range(GROUP):
                        gather(y_dram, slot, half, GROUP * s + j, gathered[slot])

            pool.wait_ge(first_in, 16)
            for slot in range(EARLY):
                for j in range(GROUP):
                    gather(x_rows, slot, slot // GROUPS, GROUP * (slot % GROUPS) + j, gathered[slot])
            for k in range(YRING):
                pool.wait_ge(y_stored[k], 16 * (YGROUPS // YRING))
            with pool.Fori(1, NB // 2) as i:
                gather_block(i, 0)
                gather_block(i, 1)

            pool.wait_ge(prep, PREP)
            broken = pool.value_load(violation[0:1, 0:1], min_val=0, max_val=1)
            with pool.If(broken != 0):
                with pool.Fori(1, NB + 1) as n:
                    pool.wait_ge(y_stored[0], 16 * (YGROUPS // YRING))
                    pool.wait_ge(g_idx, n)
                    for s in range(GROUPS):
                        for j in range(GROUP):
                            gather(y_dram, s, 0, GROUP * s + j, g_gathered)
            with pool.Else():
                pool.nop()

        @block.tensor
        def _(pe):
            pe.wait_ge(wm_in, 16)
            with pe.Fori(0, YGROUPS // YRING) as i:
                for k in range(YRING):
                    g = YRING * i + k
                    pe.wait_ge(xt_in[k], 16 * (i + 1))
                    pe.wait_ge(y_ready, YRING * i)
                    for j in range(GROUP):
                        last = pe.matmul(banks[:, k, j * F:(j + 1) * F], xT_in[:, k, j * P:(j + 1) * P], wm[:, 0, :],
                                         start=True, stop=True)
                    last.then_inc(y_product, 1)
            pe.wait_ge(const_made, CONSTS)
            pe.wait_ge(ident_made, 1)
            for group in range(EARLY):
                pe.wait_ge(gathered[group], 16 * GROUP)
                if group >= 2:
                    pe.wait_ge(turned_back, group - 1)
                for j in range(GROUP):
                    last = pe.transpose(banks[:, 6 + group % 2, j * P:(j + 1) * P], rows[:, group, j * F:(j + 1) * F],
                                        ident[:, :])
                last.then_inc(turned, 1)
            pe.wait_ge(y_ready, YGROUPS)
            pe.wait_ge(consts_in, 16 * 4)

            def edge_products(s, edges, early=None):
                for j in range(GROUP):
                    tile = GROUP * s + j
                    z = zp[:, s, j * F:(j + 1) * F]
                    last = pe.matmul(z, edges[:, tile * P:(tile + 1) * P], wm[:, 1, :], start=True, stop=early is None)
                    if early is not None:
                        last = pe.matmul(z, rows[:, early, j * P:(j + 1) * P], wm[:, 0, :], start=False, stop=True)
                return last

            def window_sums(bank_sum, bank_count, s, hot, first=True, final=True):
                for j in range(GROUP):
                    pe.matmul(bank_sum, msg[:, s, j * F:(j + 1) * F], hot[:, j, :],
                              start=(first and j == 0), stop=(final and j == GROUP - 1), skip_group_check=True)
                for j in range(GROUP):
                    last = pe.matmul(bank_count, ones[:, :], hot[:, j, :].bitcast(BF16)[:, 1::2],
                                     start=(first and j == 0), stop=(final and j == GROUP - 1), skip_group_check=True)
                return last

            def sum_group(group, s, peeled):
                bank = s % 2
                pe.wait_ge(relu_done, group + 1)
                pe.wait_ge(onehot_ready, group + 1)
                if not (peeled and group < 2):
                    pe.wait_ge(acc_done, group - 1)
                window_sums(sums[:, bank, 0:WINDOW], sums[:, bank, WINDOW:2 * WINDOW], s, onehot[:, s, :, :])\
                    .then_inc(sums_ready, 1)

            def update(n, h_bank, x_t, mean_t, tiles, landed, landed_at):
                pe.wait_ge(landed, landed_at)
                for t in range(tiles):
                    nodes = slice(t * NT, (t + 1) * NT)
                    h = hp[0:NT, h_bank, t * F:(t + 1) * F]
                    pe.matmul(h, x_t[:, nodes], wu[:, 0, :], start=True, stop=False, skip_group_check=True)
                    if t == 0:
                        pe.wait_ge(upd_step, STEPS * n + 3)
                    last = pe.matmul(h, mean_t[:, nodes], wu[:, 1, :], start=False, stop=True, skip_group_check=True)
                last.then_inc(h_ready, 1)

            def run_block(i, half, peeled):
                b = block_of(i, half)
                for s in range(GROUPS):
                    group = GROUPS * b + s
                    if s == 0:
                        pe.wait_ge(edges_in[half], 16 * (i + 1))
                    if not (peeled and group < 4):
                        pe.wait_ge(added[GROUPS * (1 - half) + s], i + half)
                    if peeled:
                        pe.wait_ge(turned_back, group + 1)
                    edge_products(s, edge_buf[:, half, :], early=group if peeled else None).then_inc(z_ready, 1)
                    if not (peeled and group < 1):
                        sum_group(group - 1, (s - 1) % GROUPS, peeled)
                    if s == 2 and not peeled:
                        update(b - LAG, half, xT_buf[:, half, :], meanT, 1, node_in[half], 32 * i)

            run_block(0, 0, True)
            run_block(0, 1, True)
            with pe.Fori(1, NB // 2) as i:
                run_block(i, 0, False)
                run_block(i, 1, False)
            sum_group(NS - 1, GROUPS - 1, False)
            update(UPDATES - 1, 0, xT_last, mean_last, REST, last_in, 32)

            broken = pe.value_load(violation[0:1, 0:1], min_val=0, max_val=1)
            with pe.If(broken != 0):
                with pe.Fori(0, NB) as b:
                    pe.wait_ge(g_edges_in, 16 * (b + 1))
                    for s in range(GROUPS):
                        pe.wait_ge(g_added, GROUPS * b)
                        edge_products(s, edge_buf[:, 0, :]).then_inc(g_z, 1)
                    with pe.Fori(0, NWIDE) as w:
                        pe.wait_ge(g_relu, GROUPS * (b + 1))
                        pe.wait_ge(g_acc, b * NWIDE + w)
                        for s in range(GROUPS):
                            pe.wait_ge(g_onehot, (b * NWIDE + w) * GROUPS + s + 1)
                            window_sums(sums[:, 0, :], sums[:, 1, :], s, wide_onehot, first=(s == 0),
                                        final=(s == GROUPS - 1)).then_inc(g_used, 1)
                with pe.Fori(0, NTILES) as t:
                    update(t + UPDATES, 0, xT_buf[:, 0, :], meanT, 1, g_node_in, 32 * (t + 1))
            with pe.Else():
                pe.nop()

        @block.vector
        def _(dve):
            step = [0]

            def prepared(ins):
                step[0] += 1
                ins.then_inc(prep, 1)
                dve.wait_ge(prep, step[0])

            def bias_y(i, k, peeled):
                dve.wait_ge(y_product, YRING * i + k + 1)
                if not peeled:
                    dve.wait_ge(y_stored[k], 16 * i)
                dve.tensor_tensor(y_out[:, k, :].rearrange("p (j f) -> p j f", f=F),
                                  banks[:, k, :].rearrange("p (j f) -> p j f", f=F),
                                  bias_msg[:, :].unsqueeze(1).to_broadcast([P, GROUP, F]), ALU.add).then_inc(y_ready, 1)

            dve.wait_ge(const_made, CONSTS)
            prepared(dve.tensor_copy(iota_f[:, :], iota_i[:, :]))
            prepared(dve.tensor_copy(done_f[:, :], done_nodes[:, :]))
            dve.tensor_scalar(ident[:, :], ident_i, 0.0, None, ALU.is_equal).then_inc(ident_made, 1)
            dve.wait_ge(bias_in, 16)
            bias_y(0, 0, True)
            dve.wait_ge(dstrow_in, 16)
            prepared(dve.tensor_copy(dst_f, dst_row[0:NB, :].rearrange("p (g e) -> p g e", g=GROUPS)))
            bias_y(0, 1, True)
            prepared(dve.tensor_reduce(least[0:NB, :], dst_f, AX.X, ALU.min))
            bias_y(0, 2, True)
            prepared(dve.tensor_reduce(most[0:NB, :], dst_f, AX.X, ALU.max))
            bias_y(0, 3, True)
            prepared(dve.tensor_scalar(late[0:NB, :], least[0:NB, :], -1.0, done_f[0:NB, 0:1], ALU.mult, ALU.add))
            prepared(dve.tensor_tensor(wide[0:NB, :], most[0:NB, :], least[0:NB, :], ALU.subtract))
            prepared(dve.scalar_tensor_tensor(wide[0:NB, :], wide[0:NB, :], float(1 - WINDOW), late[0:NB, :],
                                              ALU.add, ALU.max))
            prepared(dve.tensor_copy(found[0:NB, 0:GROUPS], least[0:NB, :]))
            prepared(dve.tensor_scalar(found[0:NB, GROUPS:2 * GROUPS], wide[0:NB, :], 0.0, None, ALU.is_gt))
            assert step[0] == PREP - 3
            bias_y(0, 4, True)
            with dve.Fori(1, YGROUPS // YRING) as i:
                for k in range(YRING):
                    bias_y(i, k, False)

            dve.wait_ge(idx_in, 32)
            dve.wait_ge(spans_in, 16)
            prepared(dve.tensor_tensor(dst_rel[:, :, :, :],
                                       dst_idx[:, :, :].rearrange("p b (g j) -> p b g j", g=GROUPS),
                                       spans[:, :, 0:GROUPS].unsqueeze(3).to_broadcast([P, NB, GROUPS, GROUP]),
                                       ALU.subtract))
            prepared(dve.tensor_reduce(violation[0:1, 0:1], spans[0:1, :, GROUPS:2 * GROUPS], AX.XY, ALU.max))
            prepared(dve.memset(stats[:, :, :, :], 0.0))
            dve.wait_ge(consts_in, 16 * 4)
            assert step[0] == PREP

            def make_onehot(i, half, s, peeled):
                b = block_of(i, half)
                if not (peeled and half == 0):
                    dve.wait_ge(sums_ready, GROUPS * (b - 1) + s + 1)
                dve.tensor_tensor(onehot[:, s, :, :],
                                  iota_f[:, 0:WINDOW].unsqueeze(1).to_broadcast([P, GROUP, WINDOW]),
                                  dst_rel[:, b, s, :].unsqueeze(2).to_broadcast([P, GROUP, WINDOW]),
                                  ALU.is_equal).then_inc(onehot_ready, 1)

            def accumulate(group, s, base, peeled):
                dve.wait_ge(sums_ready, group + 1)
                if peeled and group == 0:
                    dve.wait_ge(acc_zeroed, 3)
                else:
                    dve.wait_ge(acc_done, group)
                dve.tensor_tensor(acc[:, :, bass.ds(base, WINDOW)], acc[:, :, bass.ds(base, WINDOW)],
                                  sums[:, s % 2, 0:2 * WINDOW].rearrange("p (a w) -> p a w", a=2),
                                  ALU.add).then_inc(acc_done, 1)

            def base_of(b, s):
                return dve.value_load(spans[0:1, b, s:s + 1], min_val=0, max_val=n_nodes)

            def update_steps(n, t0, tiles, h_bank, x_t, xb, r, done, mean, inverse, stats_sems, stats_at):
                at = [0]

                def wait():
                    dve.wait_ge(upd_step, STEPS * n + at[0])

                def did(ins):
                    ins.then_inc(upd_step, 1)
                    at[0] += 1

                def each_row(row):
                    return row[0:NT, :].unsqueeze(1).to_broadcast([NT, tiles, F])

                h = hp[0:NT, h_bank, 0:tiles * F].rearrange("p (t f) -> p t f", f=F)
                x_t, xb, r, done = (v[0:NT, :, :] for v in (x_t, xb, r, done))
                total, count = (acc[:, k, bass.ds(t0 * NT, tiles * NT)] for k in range(2))

                def moments_of(which):
                    wait()
                    for t in range(tiles):
                        ins = dve.bn_stats(stats[0:NT, which, t, :], r[:, t, :])
                    ins.then_inc(stats_sems[which], 1)
                    dve.wait_ge(const_made, CONSTS)
                    dve.wait_ge(stats_sems[which], stats_at)
                    for t in range(tiles):
                        ins = dve.bn_aggr(moments[0:NT, which, t, :], stats[0:NT, which, t, :])
                    ins.then_inc(moments_ready, 1)

                def invert(which):
                    dve.wait_ge(sqrt_done, 2 * n + which + 1)
                    did(dve.reciprocal(rstd[0:NT, which, 0:tiles], stdev[0:NT, which, 0:tiles]))

                def first():
                    did(dve.tensor_scalar(inverse, count, 1.0, None, ALU.max))
                    wait()
                    did(dve.reciprocal(inverse, inverse))
                    wait()
                    did(dve.tensor_tensor(mean, total, inverse, ALU.mult))

                def second(landed, landed_at):
                    dve.wait_ge(landed, landed_at)
                    did(dve.tensor_tensor(xb, x_t, each_row(beta_b), ALU.add))
                    dve.wait_ge(h_ready, n + 1)
                    did(dve.tensor_tensor(r, h, each_row(bias_upd), ALU.add))
                    moments_of(0)

                def third():
                    invert(0)
                    for t in range(tiles):
                        ins = dve.scalar_tensor_tensor(r[:, t, :], r[:, t, :], moments[0:NT, 0, t, 0:1], gamma_b[0:NT, :],
                                                       ALU.subtract, ALU.mult)
                    did(ins)
                    wait()
                    for t in range(tiles):
                        ins = dve.scalar_tensor_tensor(r[:, t, :], r[:, t, :], rstd[0:NT, 0, t:t + 1], xb[:, t, :],
                                                       ALU.mult, ALU.add)
                    did(ins)
                    wait()
                    did(dve.scalar_tensor_tensor(r, r, 0.0, x_t, ALU.max, ALU.add))
                    moments_of(1)

                def fourth(stored=None, stored_at=0):
                    invert(1)
                    wait()
                    if stored is not None:
                        dve.wait_ge(stored, stored_at)
                    for t in range(tiles):
                        ins = dve.tensor_scalar(done[:, t, :], r[:, t, :], moments[0:NT, 1, t, 0:1],
                                                rstd[0:NT, 1, t:t + 1], ALU.subtract, ALU.mult)
                    did(ins)
                    assert at[0] == STEPS, at[0]

                return first, second, third, fourth

            def update_tile(n, t, slot, stats_sems, stats_at):
                return update_steps(n, t, 1, slot, x_buf[:, slot, :, :], xbeta, hid, out_buf[:, slot, :, :],
                                    meanT[:, :], inv[:, :], stats_sems, stats_at)

            def run_block(i, half, peeled):
                b = block_of(i, half)
                if not peeled:
                    first, second, third, fourth = update_tile(b - LAG, b - LAG, half,
                                                               stats_ready[2 * half:2 * half + 2], i)
                for s in range(GROUPS):
                    group = GROUPS * b + s
                    slot = GROUPS * half + s
                    make_onehot(i, half, s, peeled)
                    if s == 1 and not peeled:
                        dve.wait_ge(acc_done, GROUPS * b)
                        first()
                    dve.wait_ge(z_ready, group + 1)
                    dve.wait_ge(gathered[slot], 16 * GROUP * (i + 1))
                    if peeled:
                        ins = dve.tensor_tensor(msg[:, s, :].rearrange("p (j f) -> p j f", f=F),
                                                zp[:, s, :].rearrange("p (j f) -> p j f", f=F),
                                                bias_msg[:, :].unsqueeze(1).to_broadcast([P, GROUP, F]), ALU.add)
                    else:
                        ins = dve.tensor_tensor(msg[:, s, :], zp[:, s, :], rows[:, slot, :], ALU.add)
                    ins.then_inc(added[slot], 1)
                    if s == 1 and not peeled:
                        dve.wait_ge(upd_step, STEPS * (b - LAG) + 3)
                    if not (peeled and group == 0):
                        accumulate(group - 1, (s - 1) % GROUPS, base_of(b, s - 1) if s else base_of(b - 1, GROUPS - 1), peeled)
                    if s == 2 and not peeled:
                        second(node_in[half], 32 * i)
                    if s == 3 and not peeled:
                        third()
                        fourth(out_stored[half], 16 * (i - 1))
                dve.tensor_copy(gather_idx[:, half, :], src_idx[:, b + 2, :]).then_inc(idx_ready[half], 1)

            run_block(0, 0, True)
            run_block(0, 1, True)
            with dve.Fori(1, NB // 2) as i:
                run_block(i, 0, False)
                run_block(i, 1, False)
            accumulate(NS - 1, (NS - 1) % GROUPS, base_of(NB - 1, GROUPS - 1), False)
            dve.wait_ge(acc_done, NS)
            first, second, third, fourth = update_steps(
                UPDATES - 1, NB - LAG, REST, 0, x_last, xbeta_last, hid_last, hid_last, mean_last, inv_last,
                last_stats, 1)
            first()
            second(last_in, 32)
            third()
            fourth()

            broken = dve.value_load(violation[0:1, 0:1], min_val=0, max_val=1)
            with dve.If(broken != 0):
                dve.wait_ge(upd_step, STEPS * UPDATES)
                dve.wait_ge(last_stored, 16)
                dve.memset(acc[:, :, :], 0.0).then_inc(g_start, 1)
                dve.wait_ge(g_start, 1)
                with dve.Fori(0, NB) as b:
                    dve.tensor_copy(gather_idx[:, 0, :], src_idx[:, b, :]).then_inc(g_idx, 1)
                    for s in range(GROUPS):
                        dve.wait_ge(g_z, GROUPS * b + s + 1)
                        dve.wait_ge(g_gathered, 16 * TILES * (b + 1))
                        dve.wait_ge(g_used, NWIDE * GROUPS * b)
                        dve.tensor_tensor(msg[:, s, :], zp[:, s, :], rows[:, s, :], ALU.add).then_inc(g_added, 1)
                    dve.tensor_copy(wide_dst[:, :], dst_idx[:, b, :]).then_inc(g_dst, 1)
                    with dve.Fori(0, NWIDE) as w:
                        dve.wait_ge(g_dst, b * (NWIDE + 1) + w + 1)
                        for s in range(GROUPS):
                            dve.wait_ge(g_used, (b * NWIDE + w) * GROUPS + s)
                            dve.tensor_tensor(wide_onehot,
                                              iota_f[:, :].unsqueeze(1).to_broadcast([P, GROUP, WIDE]),
                                              wide_dst[:, GROUP * s:GROUP * (s + 1)].unsqueeze(2)
                                              .to_broadcast([P, GROUP, WIDE]), ALU.is_equal).then_inc(g_onehot, 1)
                        dve.wait_ge(g_onehot, (b * NWIDE + w) * GROUPS + GROUPS)
                        dve.tensor_scalar(wide_dst[:, :], wide_dst[:, :], float(WIDE), None, ALU.subtract)\
                            .then_inc(g_dst, 1)
                        dve.wait_ge(g_used, (b * NWIDE + w) * GROUPS + GROUPS)
                        dve.wait_ge(g_acc, b * NWIDE + w)
                        dve.tensor_tensor(acc[:, :, bass.ds(w * WIDE, WIDE)], acc[:, :, bass.ds(w * WIDE, WIDE)],
                                          sums[:, :, :], ALU.add).then_inc(g_acc, 1)
                dve.wait_ge(g_acc, NB * NWIDE)
                with dve.Fori(1, NTILES + 1) as m:
                    t = m - 1
                    first, second, third, fourth = update_tile(t + UPDATES, t, 0, g_stats, m)
                    first()
                    second(g_node_in, 32 * m)
                    third()
                    fourth(g_stored, 16 * t)
            with dve.Else():
                dve.nop()


def kernel(x, src, dst, edge_attr_128, L0_gnn_W_msg, L0_gnn_b_msg, L0_gnn_W_upd, L0_gnn_b_upd, L0_gnn_gamma,
           L0_gnn_beta):
    import numpy as np
    import concourse.bacc as bacc
    from concourse.bass_utils import run_bass_kernel_spmd

    x, src, dst, edges = (np.asarray(a) for a in (x, src, dst, edge_attr_128))
    n, f = x.shape
    e = src.shape[0]
    NB, NT, NTILES, COLS, _ = sizes(n, e)

    xT = np.zeros((f, COLS), x.dtype)
    xT[:, :n] = x.T
    x_rows = np.zeros((NTILES * NT, f), x.dtype)
    x_rows[:n] = x
    edges_p = np.zeros((NB * BLOCK, f), edges.dtype)
    edges_p[:e] = edges
    src_p = np.zeros(((NB + 2) * BLOCK,), src.dtype)
    src_p[:e] = src
    dst_p = np.full((NB * BLOCK,), n, dst.dtype)
    dst_p[:e] = dst
    arrays = {
        "xT": xT,
        "x_rows": x_rows,
        "edgesT": np.ascontiguousarray(edges_p.reshape(NB, BLOCK, f).transpose(0, 2, 1)),
        "src_tiles": np.ascontiguousarray(src_p.reshape(NB + 2, TILES, P).transpose(2, 0, 1)),
        "dst_tiles": np.ascontiguousarray(dst_p.reshape(NB, TILES, P).transpose(2, 0, 1)),
        "dst_rows": dst_p.reshape(NB, BLOCK),
        "w_msg": np.asarray(L0_gnn_W_msg),
        "b_msg": np.asarray(L0_gnn_b_msg),
        "w_upd": np.asarray(L0_gnn_W_upd),
        "b_upd": np.asarray(L0_gnn_b_upd),
        "gamma": np.asarray(L0_gnn_gamma),
        "beta": np.asarray(L0_gnn_beta),
    }
    nc = bacc.Bacc("TRN2", target_bir_lowering=False, num_devices=1)
    args = [nc.dram_tensor(name, a.shape, mybir.dt.from_np(a.dtype), kind="ExternalInput").ap()
            for name, a in arrays.items()]
    out = nc.dram_tensor("out", (NTILES * NT, f), mybir.dt.float32, kind="ExternalOutput").ap()
    graph_layer(nc, *args, out, n, e)
    r = run_bass_kernel_spmd(nc, [arrays], core_ids=[0])
    return r.results[0]["out"][:n]
```

```python
from contextlib import ExitStack

import concourse.bass as bass
from concourse import mybir

P = 128
TILES = 16
GROUP = 4
GROUPS = TILES // GROUP
BLOCK = TILES * P
RING = 2 * GROUPS
LAG = 2
WIDE = 512
YRING = 5
EARLY_BLOCKS = 3
EARLY = EARLY_BLOCKS * GROUPS
YBANKS = (4, 5, 6, 4, 5)
FIRST = 4
LISTED = 6
EPS = 1e-5

ALU = mybir.AluOpType
ACT = mybir.ActivationFunctionType
F32 = mybir.dt.float32
I32 = mybir.dt.int32
U32 = mybir.dt.uint32
BF16 = mybir.dt.bfloat16
AX = mybir.AxisListType


def sizes(n_nodes, n_edges):
    blocks = -(-n_edges // (2 * BLOCK)) * 2
    node_tile = min(P, n_nodes // blocks)
    tiles = -(-n_nodes // node_tile)
    per_pass = WIDE * YRING
    columns = -(-(n_nodes + P) // per_pass) * per_pass
    window = -(-(3 * GROUP * P * n_nodes) // (2 * n_edges) // 16) * 16
    return blocks, node_tile, tiles, columns, max(16, min(window, P))


def graph_layer(nc, xT, x_rows, edgesT, src_tiles, dst_tiles, dst_rows, w_msg, b_msg, w_upd, b_upd, gamma, beta,
                out, n_nodes, n_edges):
    NB, NT, NTILES, COLS, WINDOW = sizes(n_nodes, n_edges)
    F = w_msg.shape[1]
    REST = NTILES - (NB - LAG)
    STAGED = YRING * WIDE
    assert F == P and 0 < REST and REST * F <= 512 and COLS >= 4 * STAGED
    assert NB >= LISTED + 4 and (NB - FIRST) * TILES >= (GROUPS - 1) * GROUP * F
    NS = NB * GROUPS
    NWIDE = COLS // WIDE
    YGROUPS = COLS // WIDE

    y_dram = nc.dram_tensor("y_rows", [COLS, F], F32).ap()
    spans_dram = nc.dram_tensor("spans_of_blocks", [NB, 2 * GROUPS], I32).ap()

    with ExitStack() as ctx:
        def sb(name, shape, dt=F32):
            return ctx.enter_context(nc.sbuf_tensor(name, shape, dt))

        def sem(name):
            return ctx.enter_context(nc.semaphore(name))

        acc = sb("acc", [P, 2, COLS])
        edge_buf = sb("edge_buf", [P, 2, BLOCK])
        rows = sb("rows", [P, RING, GROUP * F])
        msg = sb("msg", [P, GROUPS, GROUP * F])
        onehot = sb("onehot", [P, GROUPS, GROUP, WINDOW])
        src_idx = sb("src_idx", [P, NB, TILES], I32)
        first_idx = sb("first_idx", [P, LISTED, TILES], I32)
        gather_idx = sb("gather_idx", [P, 2, TILES], I32)
        dst_idx = sb("dst_idx", [P, NB, TILES], I32)
        dst_rel = sb("dst_rel", [P, NB, GROUPS, GROUP])
        spans = sb("spans", [P, NB, 2 * GROUPS], I32)
        iota_i = sb("iota_i", [P, WIDE], I32)
        iota_f = sb("iota_f", [P, WIDE])
        wm = sb("wm", [P, 2, F])
        wu = sb("wu", [P, 2, F])
        bias_msg = sb("bias_msg", [P, F])
        bias_upd = sb("bias_upd", [P, F])
        gamma_b = sb("gamma_b", [P, F])
        beta_b = sb("beta_b", [P, F])
        ones = sb("ones", [P, P], BF16)
        least = sb("least", [P, GROUPS])
        most = sb("most", [P, GROUPS])
        done_nodes = sb("done_nodes", [P, 1], I32)
        done_f = sb("done_f", [P, 1])
        late = sb("late", [P, GROUPS])
        wide = sb("wide", [P, GROUPS])
        found = sb("found", [P, 2 * GROUPS], I32)
        violation = sb("violation", [1, 1], I32)
        xT_buf = sb("xT_buf", [P, 2, NT])
        x_buf = sb("x_buf", [P, 2, 1, F])
        meanT = sb("meanT", [P, NT])
        inv = sb("inv", [P, NT])
        hid = sb("hid", [P, 1, F])
        xbeta = sb("xbeta", [P, 1, F])
        out_buf = sb("out_buf", [P, 2, 1, F])
        stats = sb("stats", [P, 2, REST, 6])
        moments = sb("moments", [P, 2, REST, 2])
        stdev = sb("stdev", [P, 2, REST])
        rstd = sb("rstd", [P, 2, REST])
        eps = sb("eps", [P, 1])
        zeros = sb("zeros", [P, 1])
        ident = sb("ident", [P, P])
        wide_dst = sb("wide_dst", [P, TILES])
        dst_row = sb("dst_row", [P, BLOCK], I32)
        xT_in = acc[:, 1, COLS - 2 * STAGED:COLS - STAGED].rearrange("p (k n) -> p k n", k=YRING)
        y_out = acc[:, 1, COLS - STAGED:COLS].rearrange("p (k n) -> p k n", k=YRING)
        dst_f = msg[:, :, :].rearrange("p a b -> p (a b)")[0:NB, 0:BLOCK].rearrange("p (g e) -> p g e", g=GROUPS)
        wide_onehot = dst_row[:, :].bitcast(F32).rearrange("p (k n) -> p k n", k=GROUP)
        last = dst_row[:, :].bitcast(F32)
        RF, RN = REST * F, REST * NT
        x_last, xbeta_last, hid_last = (last[:, k * RF:(k + 1) * RF].rearrange("p (t f) -> p t f", f=F) for k in range(3))
        xT_last, inv_last = (last[:, 3 * RF + k * RN:3 * RF + (k + 1) * RN] for k in range(2))
        ident_i = x_buf[:, 0, 0, :].bitcast(I32)
        mean_last = iota_i[:, :].bitcast(F32)[:, 0:RN]

        rel = dst_rel[:, :, :, :].rearrange("p b g j -> p (b g j)")
        early_rows = [rows[:, GROUPS + s, :] for s in range(GROUPS)]
        early_rows += [last[:, s * GROUP * F:(s + 1) * GROUP * F] for s in range(GROUPS)]
        early_turned = early_rows + [rel[:, FIRST * TILES + s * GROUP * F:FIRST * TILES + (s + 1) * GROUP * F]
                                     for s in range(GROUPS - 1)]
        early_rows += [rows[:, s, :] for s in range(GROUPS)]
        early_turned += early_rows[-1:]

        banks = ctx.enter_context(nc.psum_tensor("banks", [P, 8, 512], F32))
        zp = banks[:, 0:4, :]
        sums = banks[:, 4:6, :]
        hp = banks[:, 6:8, :]

        wm_in = sem("wm_in")
        bias_in = sem("bias_in")
        consts_in = sem("consts_in")
        first_in = sem("first_in")
        src_in = sem("src_in")
        first_dst_in = sem("first_dst_in")
        dst_in = sem("dst_in")
        dst_rel_made = sem("dst_rel_made")
        dstrow_in = sem("dstrow_in")
        spans_out = sem("spans_out")
        spans_in = sem("spans_in")
        xt_in = [sem(f"xt_in{k}") for k in range(YRING)]
        y_stored = [sem(f"y_stored{k}") for k in range(YRING)]
        y_product = sem("y_product")
        y_ready = sem("y_ready")
        const_made = sem("const_made")
        prep = sem("prep")
        acc_zeroed = sem("acc_zeroed")
        y_out_zeroed = sem("y_out_zeroed")
        early_in = [sem(f"early_in{k}") for k in range(EARLY)]
        turned = sem("turned")
        turned_back = sem("turned_back")
        idx_ready = [sem(f"idx_ready{k}") for k in range(RING)]
        edges_in = [sem(f"edges_in{k}") for k in range(2)]
        gathered = [sem(f"gathered{k}") for k in range(RING)]
        z_ready = sem("z_ready")
        onehot_ready = sem("onehot_ready")
        added = [sem(f"added{k}") for k in range(RING)]
        relu_done = sem("relu_done")
        sums_ready = sem("sums_ready")
        acc_done = sem("acc_done")
        node_in = [sem(f"node_in{k}") for k in range(2)]
        last_in = sem("last_in")
        last_stats = [sem(f"last_stats{k}") for k in range(2)]
        last_stored = sem("last_stored")
        upd_step = sem("upd_step")
        ident_made = sem("ident_made")
        h_ready = sem("h_ready")
        moments_ready = sem("moments_ready")
        stats_ready = [sem(f"stats_ready{k}") for k in range(4)]
        sqrt_done = sem("sqrt_done")
        out_stored = [sem(f"out_stored{k}") for k in range(2)]
        g_start = sem("g_start")
        g_edges_in = sem("g_edges_in")
        g_idx = sem("g_idx")
        g_gathered = sem("g_gathered")
        g_z = sem("g_z")
        g_added = sem("g_added")
        g_relu = sem("g_relu")
        g_dst = sem("g_dst")
        g_onehot = sem("g_onehot")
        g_used = sem("g_used")
        g_stats = [sem(f"g_stats{k}") for k in range(2)]
        g_acc = sem("g_acc")
        g_node_in = sem("g_node_in")
        g_stored = sem("g_stored")

        block = ctx.enter_context(nc.Block())

        CONSTS = 6
        PREP = 13
        STEPS = 11
        UPDATES = NB - LAG + 1

        def turn_bank(group):
            return 7 if group < GROUPS else 6 + group % 2

        def early_after(i, k):
            return {1: 0, 3: 1}[k] + 2 * (i - (YGROUPS // YRING - 2)) if k in (1, 3) else None

        def tiles_with_edges(group):
            return max(0, min(GROUP, -(-n_edges // P) - GROUP * group))

        def block_of(i, half):
            return 2 * i + half


        def node_load(sp, t, slot, landed):
            sp.dma_start(xT_buf[:, slot, :], xT[:, bass.ds(t * NT, NT)]).then_inc(landed, 16)
            sp.dma_start(x_buf[0:NT, slot, 0, :], x_rows[bass.ds(t * NT, NT), :]).then_inc(landed, 16)

        def node_store(sp, t, slot, stored):
            sp.dma_start(out[bass.ds(t * NT, NT), :], out_buf[0:NT, slot, 0, :]).then_inc(stored, 16)

        @block.sync
        def _(sp):
            sp.dma_start(wm[:, :, :], w_msg.rearrange("(a p) n -> p a n", p=P)).then_inc(wm_in, 16)
            for k in range(YRING):
                sp.dma_start(xT_in[:, k, :], xT[:, k * WIDE:(k + 1) * WIDE]).then_inc(xt_in[k], 16)

            def store_y(i, k):
                g = YRING * i + k
                sp.wait_ge(y_ready, g + 1)
                sp.dma_start(y_dram[bass.ds(g * WIDE, WIDE), :].rearrange("(j p) f -> p j f", p=P),
                             y_out[:, k, :].rearrange("p (j f) -> p j f", f=F)).then_inc(y_stored[k], 16)

            def y_round(i):
                for k in range(YRING):
                    sp.wait_ge(y_product, YRING * i + k - YRING + 1)
                    sp.dma_start(xT_in[:, k, :], xT[:, bass.ds((YRING * i + k) * WIDE, WIDE)]).then_inc(xt_in[k], 16)
                    store_y(i - 1, k)

            with sp.Fori(1, YGROUPS // YRING - 2) as i:
                y_round(i)
            sp.dma_start(edge_buf[:, 0, :], edgesT[0, :, :]).then_inc(edges_in[0], 16)
            for i in range(YGROUPS // YRING - 2, YGROUPS // YRING):
                y_round(i)
            for k in range(YRING):
                store_y(YGROUPS // YRING - 1, k)
            sp.dma_start(edge_buf[:, 1, :], edgesT[1, :, :]).then_inc(edges_in[1], 16)

            def fetch(i, half, least):
                b = block_of(i, half)
                sp.wait_ge(z_ready, GROUPS * (b - 2) + GROUPS)
                sp.dma_start(edge_buf[:, half, :], edgesT[b, :, :]).then_inc(edges_in[half], 16)
                if least > 1:
                    sp.wait_ge(upd_step, STEPS * (b - 3))
                    node_store(sp, b - 4, half, out_stored[half])
                node_load(sp, b - 2, half, node_in[half])

            fetch(1, 0, 1)
            fetch(1, 1, 1)
            with sp.Fori(2, NB // 2) as i:
                fetch(i, 0, 2)
                fetch(i, 1, 2)
            t0 = NB - LAG
            sp.dma_start(xT_last, xT[:, t0 * NT:NTILES * NT]).then_inc(last_in, 16)
            sp.dma_start(x_last[0:NT, :, :], x_rows[t0 * NT:NTILES * NT, :].rearrange("(t p) f -> p t f", p=NT))\
              .then_inc(last_in, 16)
            for t in (t0 - 2, t0 - 1):
                sp.wait_ge(upd_step, STEPS * (t + 1))
                node_store(sp, t, t % 2, out_stored[t % 2])
            sp.wait_ge(upd_step, STEPS * UPDATES)
            sp.dma_start(out[t0 * NT:NTILES * NT, :].rearrange("(t p) f -> p t f", p=NT), hid_last[0:NT, :, :])\
              .then_inc(last_stored, 16)
            for slot in range(2):
                sp.wait_ge(out_stored[slot], 16 * (t0 // 2))
            sp.wait_ge(last_stored, 16)

            broken = sp.value_load(violation[0:1, 0:1], min_val=0, max_val=1)
            with sp.If(broken != 0):
                sp.nop().then_inc(g_stored, 16)
                with sp.Fori(0, NB) as b:
                    sp.wait_ge(g_start, 1)
                    sp.wait_ge(g_z, GROUPS * b + 1)
                    sp.dma_start(edge_buf[:, 0, :], edgesT[b, :, :]).then_inc(g_edges_in, 16)
                with sp.Fori(0, NTILES) as t:
                    node_load(sp, t, 0, g_node_in)
                    sp.wait_ge(upd_step, STEPS * (t + UPDATES + 1))
                    node_store(sp, t, 0, g_stored)
                sp.wait_ge(g_stored, 16 * NTILES + 16)
            with sp.Else():
                sp.nop()

        @block.scalar
        def _(act):
            act.dma_start(first_idx[:, :, :], src_tiles[:, 0:LISTED, :]).then_inc(first_in, 16)
            act.dma_start(dst_row[0:NB, :], dst_rows).then_inc(dstrow_in, 16)
            act.dma_start(bias_msg[:, :], b_msg.partition_broadcast(P)).then_inc(bias_in, 16)
            act.dma_start(dst_idx[:, 0:FIRST, :], dst_tiles[:, 0:FIRST, :]).then_inc(first_dst_in, 16)

            def zero(columns):
                act.activation(columns, zeros[:, :].to_broadcast([P, columns.shape[1]]), ACT.Copy).then_inc(acc_zeroed, 1)

            def turn_back(group):
                act.wait_ge(turned, group + 1)
                act.activation(early_turned[group], banks[:, turn_bank(group), :], ACT.Copy).then_inc(turned_back, 1)

            def square_root(n, which, tiles=1):
                act.wait_ge(moments_ready, 2 * n + which + 1)
                act.activation(stdev[0:NT, which, 0:tiles], moments[0:NT, which, 0:tiles, 1], ACT.Sqrt, bias=eps[0:NT, :])\
                   .then_inc(sqrt_done, 1)

            def relu(i, half, updates=True):
                b = block_of(i, half)
                for s in range(GROUPS):
                    act.wait_ge(added[GROUPS * half + s], i + 1)
                    act.activation(msg[:, s, :], msg[:, s, :], ACT.Relu).then_inc(relu_done, 1)
                    if s >= 2 and updates:
                        square_root(b - LAG, s - 2)

            act.wait_ge(const_made, CONSTS)
            zero(acc[:, 0, :])
            act.wait_ge(prep, PREP - 3)
            act.dma_start(spans_dram, found[0:NB, :]).then_inc(spans_out, 16)
            act.wait_ge(spans_out, 16)
            act.dma_start(spans[:, :, :].rearrange("p b g -> p (b g)"),
                          spans_dram.rearrange("(a b) g -> a (b g)", a=1).to_broadcast([P, NB * 2 * GROUPS]))\
               .then_inc(spans_in, 16)
            for group in range(GROUPS):
                turn_back(group)
            zero(acc[:, 1, 0:COLS - 2 * STAGED])
            relu(0, 0, updates=False)
            act.wait_ge(y_product, YGROUPS)
            zero(acc[:, 1, COLS - 2 * STAGED:COLS - STAGED])
            for group in range(GROUPS, EARLY):
                turn_back(group)

            for k in range(YRING):
                act.wait_ge(y_stored[k], 16 * (YGROUPS // YRING))
            act.dma_start(dst_idx[:, FIRST:NB, :], dst_tiles[:, FIRST:NB, :]).then_inc(dst_in, 16)
            act.dma_start(src_idx[:, :, :], src_tiles).then_inc(src_in, 16)
            act.dma_start(wu[:, :, :], w_upd.rearrange("(a p) n -> p a n", p=P)).then_inc(consts_in, 16)
            act.dma_start(bias_upd[:, :], b_upd.partition_broadcast(P)).then_inc(consts_in, 16)
            act.dma_start(gamma_b[:, :], gamma.partition_broadcast(P)).then_inc(consts_in, 16)
            act.dma_start(beta_b[:, :], beta.partition_broadcast(P)).then_inc(consts_in, 16)

            relu(0, 1, updates=False)
            relu(1, 0)
            relu(1, 1)
            with act.Fori(2, NB // 2) as i:
                relu(i, 0)
                relu(i, 1)
            square_root(UPDATES - 1, 0, REST)
            square_root(UPDATES - 1, 1, REST)

            act.wait_ge(prep, PREP)
            broken = act.value_load(violation[0:1, 0:1], min_val=0, max_val=1)
            with act.If(broken != 0):
                with act.Fori(0, NB) as b:
                    for s in range(GROUPS):
                        act.wait_ge(g_added, GROUPS * b + s + 2)
                        act.activation(msg[:, s, :], msg[:, s, :], ACT.Relu).then_inc(g_relu, 1)
                with act.Fori(0, NTILES) as t:
                    square_root(t + UPDATES, 0)
                    square_root(t + UPDATES, 1)
            with act.Else():
                act.nop()

        @block.gpsimd
        def _(pool):
            pool.iota(iota_i[:, :], [[1, WIDE]], base=0, channel_multiplier=0).then_inc(const_made, 1)
            pool.iota(done_nodes[:, :], [[0, 1]], base=NT * (1 - LAG), channel_multiplier=NT).then_inc(const_made, 1)
            pool.memset(ones[:, :], 1.0).then_inc(const_made, 1)
            pool.memset(eps[:, :], EPS).then_inc(const_made, 1)
            pool.memset(zeros[:, :], 0.0).then_inc(const_made, 1)
            pool.iota(ident_i, [[1, P]], base=0, channel_multiplier=-1).then_inc(const_made, 1)

            def gather(table, into, j, indices, tile, done):
                pool.indirect_dma_start(
                    into[:, j * F:(j + 1) * F], None, table,
                    bass.IndirectOffsetOnAxis(ap=indices[:, tile:tile + 1].bitcast(U32), axis=0)).then_inc(done, 16)

            def gather_block(n, half, group=None):
                for s in range(GROUPS):
                    slot = GROUPS * half + s
                    pool.wait_ge(y_stored[0], 16 * (YGROUPS // YRING))
                    pool.wait_ge(idx_ready[slot], n)
                    for j in range(GROUP if group is None else tiles_with_edges(group + s)):
                        gather(y_dram, rows[:, slot, :], j, gather_idx[:, half, :], GROUP * s + j, gathered[slot])

            def gather_listed(b, s):
                slot = GROUPS * (b % 2) + s
                for j in range(GROUP):
                    gather(y_dram, rows[:, slot, :], j, first_idx[:, b, :], GROUP * s + j, gathered[slot])

            pool.wait_ge(first_in, 16)
            for group in range(EARLY):
                if group == GROUPS:
                    pool.wait_ge(prep, 3)
                for j in range(GROUP):
                    gather(x_rows, early_rows[group], j, first_idx[:, group // GROUPS, :],
                           GROUP * (group % GROUPS) + j, early_in[group])
            for k in range(YRING):
                pool.wait_ge(y_stored[k], 16 * (YGROUPS // YRING))
            for s in range(GROUPS):
                pool.wait_ge(z_ready, s + 1)
                gather_listed(3, s)
            for s in range(GROUPS):
                if s < GROUPS - 1:
                    pool.wait_ge(turned, 2 * GROUPS + s + 1)
                else:
                    pool.wait_ge(z_ready, EARLY)
                gather_listed(4, s)
            for s in range(GROUPS):
                pool.wait_ge(added[GROUPS + s], 2)
                gather_listed(5, s)
            pairs = (NB - LISTED) // 2
            with pool.Fori(1, pairs) as n:
                gather_block(n, 0)
                gather_block(n, 1)
            gather_block(pairs, 0, NS - 2 * GROUPS)
            gather_block(pairs, 1, NS - GROUPS)

            pool.wait_ge(prep, PREP)
            broken = pool.value_load(violation[0:1, 0:1], min_val=0, max_val=1)
            with pool.If(broken != 0):
                with pool.Fori(1, NB + 1) as n:
                    pool.wait_ge(y_stored[0], 16 * (YGROUPS // YRING))
                    pool.wait_ge(g_idx, n)
                    for s in range(GROUPS):
                        for j in range(GROUP):
                            gather(y_dram, rows[:, s, :], j, gather_idx[:, 0, :], GROUP * s + j, g_gathered)
            with pool.Else():
                pool.nop()

        @block.tensor
        def _(pe):
            pe.wait_ge(wm_in, 16)

            def y_products(i, k, fresh=False):
                pe.wait_ge(xt_in[k], 16 * (i + 1))
                if not fresh:
                    pe.wait_ge(y_ready, YRING * i + k - 1)
                for j in range(GROUP):
                    product = pe.matmul(banks[:, YBANKS[k], j * F:(j + 1) * F], xT_in[:, k, j * P:(j + 1) * P],
                                        wm[:, 0, :], start=True, stop=True)
                product.then_inc(y_product, 1)

            def turn(group):
                pe.wait_ge(early_in[group], 16 * GROUP)
                if group > 0:
                    pe.wait_ge(turned_back, group if group < GROUPS else group - 1)
                for j in range(GROUP):
                    product = pe.transpose(banks[:, turn_bank(group), j * P:(j + 1) * P],
                                           early_rows[group][:, j * F:(j + 1) * F], ident[:, :])
                product.then_inc(turned, 1)

            def edge_products(s, edges, early=None):
                for j in range(GROUP):
                    tile = GROUP * s + j
                    z = zp[:, s, j * F:(j + 1) * F]
                    last = pe.matmul(z, edges[:, tile * P:(tile + 1) * P], wm[:, 1, :], start=True, stop=early is None)
                    if early is not None:
                        last = pe.matmul(z, early_turned[early][:, j * P:(j + 1) * P], wm[:, 0, :], start=False, stop=True)
                return last

            def window_sums(bank_sum, bank_count, s, hot, first=True, final=True):
                for j in range(GROUP):
                    pe.matmul(bank_sum, msg[:, s, j * F:(j + 1) * F], hot[:, j, :],
                              start=(first and j == 0), stop=(final and j == GROUP - 1), skip_group_check=True)
                for j in range(GROUP):
                    last = pe.matmul(bank_count, ones[:, :], hot[:, j, :].bitcast(BF16)[:, 1::2],
                                     start=(first and j == 0), stop=(final and j == GROUP - 1), skip_group_check=True)
                return last

            def sum_group(group, s, first=False):
                bank = s % 2
                pe.wait_ge(relu_done, group + 1)
                pe.wait_ge(onehot_ready, group + 1)
                if not first:
                    pe.wait_ge(acc_done, group - 1)
                window_sums(sums[:, bank, 0:WINDOW], sums[:, bank, WINDOW:2 * WINDOW], s, onehot[:, s, :, :])\
                    .then_inc(sums_ready, 1)

            def update(n, h_bank, x_t, mean_t, tiles, landed, landed_at):
                pe.wait_ge(landed, landed_at)
                for t in range(tiles):
                    nodes = slice(t * NT, (t + 1) * NT)
                    h = hp[0:NT, h_bank, t * F:(t + 1) * F]
                    pe.matmul(h, x_t[:, nodes], wu[:, 0, :], start=True, stop=False, skip_group_check=True)
                    if t == 0:
                        pe.wait_ge(upd_step, STEPS * n + 3)
                    last = pe.matmul(h, mean_t[:, nodes], wu[:, 1, :], start=False, stop=True, skip_group_check=True)
                last.then_inc(h_ready, 1)

            for k in range(YRING):
                y_products(0, k, fresh=(k < 2))
            with pe.Fori(1, YGROUPS // YRING - 2) as i:
                for k in range(YRING):
                    y_products(i, k)
            pe.wait_ge(const_made, CONSTS)
            pe.wait_ge(ident_made, 1)
            for group in range(GROUPS):
                turn(group)
            for i in range(YGROUPS // YRING - 2, YGROUPS // YRING):
                for k in range(YRING):
                    y_products(i, k)
                    group = early_after(i, k)
                    if group is not None:
                        pe.wait_ge(edges_in[0], 16)
                        pe.wait_ge(turned_back, group + 1)
                        edge_products(group, edge_buf[:, 0, :], early=group).then_inc(z_ready, 1)
            pe.wait_ge(y_ready, YGROUPS)
            for group in range(GROUPS, EARLY):
                turn(group)
                if group in (5, 7):
                    sum_group((group - 5) // 2, (group - 5) // 2, first=True)
            sum_group(2, 2)

            def run_block(i, half, early=False, updates=True):
                b = block_of(i, half)
                for s in range(GROUPS):
                    group = GROUPS * b + s
                    if s == 0:
                        pe.wait_ge(edges_in[half], 16 * (i + 1))
                    pe.wait_ge(added[GROUPS * (1 - half) + s], i + half)
                    if early:
                        pe.wait_ge(turned_back, group + 1)
                    edge_products(s, edge_buf[:, half, :], early=group if early else None).then_inc(z_ready, 1)
                    sum_group(group - 1, (s - 1) % GROUPS)
                    if s == 2 and updates:
                        if early:
                            pe.wait_ge(consts_in, 16 * 4)
                        update(b - LAG, half, xT_buf[:, half, :], meanT, 1, node_in[half], 32 * i)

            run_block(0, 1, early=True, updates=False)
            run_block(1, 0, early=True)
            run_block(1, 1)
            with pe.Fori(2, NB // 2) as i:
                run_block(i, 0)
                run_block(i, 1)
            sum_group(NS - 1, GROUPS - 1)
            update(UPDATES - 1, 0, xT_last, mean_last, REST, last_in, 32)

            broken = pe.value_load(violation[0:1, 0:1], min_val=0, max_val=1)
            with pe.If(broken != 0):
                pe.nop().then_inc(g_z, 1)
                pe.nop().then_inc(g_used, 1)
                with pe.Fori(0, NB) as b:
                    pe.wait_ge(g_edges_in, 16 * (b + 1))
                    for s in range(GROUPS):
                        pe.wait_ge(g_added, GROUPS * b + 1)
                        edge_products(s, edge_buf[:, 0, :]).then_inc(g_z, 1)
                    with pe.Fori(0, NWIDE) as w:
                        pe.wait_ge(g_relu, GROUPS * (b + 1))
                        pe.wait_ge(g_acc, b * NWIDE + w + 1)
                        for s in range(GROUPS):
                            pe.wait_ge(g_onehot, (b * NWIDE + w) * GROUPS + s + 1)
                            window_sums(sums[:, 0, :], sums[:, 1, :], s, wide_onehot, first=(s == 0),
                                        final=(s == GROUPS - 1)).then_inc(g_used, 1)
                with pe.Fori(0, NTILES) as t:
                    update(t + UPDATES, 0, xT_buf[:, 0, :], meanT, 1, g_node_in, 32 * (t + 1))
            with pe.Else():
                pe.nop()

        @block.vector
        def _(dve):
            step = [0]

            def prepared(ins):
                step[0] += 1
                ins.then_inc(prep, 1)
                dve.wait_ge(prep, step[0])

            def bias_y(i, k, peeled):
                dve.wait_ge(y_product, YRING * i + k + 1)
                if not peeled:
                    dve.wait_ge(y_stored[k], 16 * i)
                dve.tensor_tensor(y_out[:, k, :].rearrange("p (j f) -> p j f", f=F),
                                  banks[:, YBANKS[k], :].rearrange("p (j f) -> p j f", f=F),
                                  bias_msg[:, :].unsqueeze(1).to_broadcast([P, GROUP, F]), ALU.add).then_inc(y_ready, 1)

            dve.wait_ge(const_made, CONSTS)
            prepared(dve.tensor_copy(iota_f[:, :], iota_i[:, :]))
            prepared(dve.tensor_copy(done_f[:, :], done_nodes[:, :]))
            dve.tensor_scalar(ident[:, :], ident_i, 0.0, None, ALU.is_equal).then_inc(ident_made, 1)
            dve.wait_ge(bias_in, 16)
            bias_y(0, 0, True)
            dve.wait_ge(dstrow_in, 16)
            prepared(dve.tensor_copy(dst_f, dst_row[0:NB, :].rearrange("p (g e) -> p g e", g=GROUPS)))
            bias_y(0, 1, True)
            prepared(dve.tensor_reduce(least[0:NB, :], dst_f, AX.X, ALU.min))
            bias_y(0, 2, True)
            prepared(dve.tensor_reduce(most[0:NB, :], dst_f, AX.X, ALU.max))
            bias_y(0, 3, True)
            prepared(dve.tensor_scalar(late[0:NB, :], least[0:NB, :], -1.0, done_f[0:NB, 0:1], ALU.mult, ALU.add))
            prepared(dve.tensor_tensor(wide[0:NB, :], most[0:NB, :], least[0:NB, :], ALU.subtract))
            prepared(dve.scalar_tensor_tensor(wide[0:NB, :], wide[0:NB, :], float(1 - WINDOW), late[0:NB, :],
                                              ALU.add, ALU.max))
            prepared(dve.tensor_copy(found[0:NB, 0:GROUPS], least[0:NB, :]))
            prepared(dve.tensor_scalar(found[0:NB, GROUPS:2 * GROUPS], wide[0:NB, :], 0.0, None, ALU.is_gt))
            assert step[0] == PREP - 3
            bias_y(0, 4, True)
            with dve.Fori(1, YGROUPS // YRING - 2) as i:
                for k in range(YRING):
                    bias_y(i, k, False)

            def early_messages(slot, s):
                dve.tensor_tensor(msg[:, s, :].rearrange("p (j f) -> p j f", f=F),
                                  zp[:, s, :].rearrange("p (j f) -> p j f", f=F),
                                  bias_msg[:, :].unsqueeze(1).to_broadcast([P, GROUP, F]), ALU.add)\
                   .then_inc(added[slot], 1)

            for i in range(YGROUPS // YRING - 2, YGROUPS // YRING):
                for k in range(YRING):
                    bias_y(i, k, False)
                    group = early_after(i, k)
                    if group is not None:
                        dve.wait_ge(z_ready, group + 1)
                        early_messages(group, group)

            def relative(first, past):
                return dve.tensor_tensor(dst_rel[:, first:past, :, :],
                                         dst_idx[:, first:past, :].rearrange("p b (g j) -> p b g j", g=GROUPS),
                                         spans[:, first:past, 0:GROUPS].unsqueeze(3)
                                         .to_broadcast([P, past - first, GROUPS, GROUP]), ALU.subtract)

            dve.wait_ge(first_dst_in, 16)
            dve.wait_ge(spans_in, 16)
            prepared(relative(0, FIRST))
            prepared(dve.tensor_reduce(violation[0:1, 0:1], spans[0:1, :, GROUPS:2 * GROUPS], AX.XY, ALU.max))
            prepared(dve.memset(stats[:, :, :, :], 0.0))
            assert step[0] == PREP

            def make_onehot(i, half, s, first=False):
                b = block_of(i, half)
                if not first:
                    dve.wait_ge(sums_ready, GROUPS * (b - 1) + s + 1)
                dve.tensor_tensor(onehot[:, s, :, :],
                                  iota_f[:, 0:WINDOW].unsqueeze(1).to_broadcast([P, GROUP, WINDOW]),
                                  dst_rel[:, b, s, :].unsqueeze(2).to_broadcast([P, GROUP, WINDOW]),
                                  ALU.is_equal).then_inc(onehot_ready, 1)

            def accumulate(group, s, base, first=False):
                dve.wait_ge(sums_ready, group + 1)
                if first:
                    dve.wait_ge(acc_zeroed, 3)
                    dve.wait_ge(y_out_zeroed, YRING)
                else:
                    dve.wait_ge(acc_done, group)
                dve.tensor_tensor(acc[:, :, bass.ds(base, WINDOW)], acc[:, :, bass.ds(base, WINDOW)],
                                  sums[:, s % 2, 0:2 * WINDOW].rearrange("p (a w) -> p a w", a=2),
                                  ALU.add).then_inc(acc_done, 1)

            def base_of(b, s):
                return dve.value_load(spans[0:1, b, s:s + 1], min_val=0, max_val=n_nodes)

            def update_steps(n, t0, tiles, h_bank, x_t, xb, r, done, mean, inverse, stats_sems, stats_at):
                at = [0]

                def wait():
                    dve.wait_ge(upd_step, STEPS * n + at[0])

                def did(ins):
                    ins.then_inc(upd_step, 1)
                    at[0] += 1

                def each_row(row):
                    return row[0:NT, :].unsqueeze(1).to_broadcast([NT, tiles, F])

                h = hp[0:NT, h_bank, 0:tiles * F].rearrange("p (t f) -> p t f", f=F)
                x_t, xb, r, done = (v[0:NT, :, :] for v in (x_t, xb, r, done))
                total, count = (acc[:, k, bass.ds(t0 * NT, tiles * NT)] for k in range(2))

                def moments_of(which):
                    wait()
                    for t in range(tiles):
                        ins = dve.bn_stats(stats[0:NT, which, t, :], r[:, t, :])
                    ins.then_inc(stats_sems[which], 1)
                    dve.wait_ge(const_made, CONSTS)
                    dve.wait_ge(stats_sems[which], stats_at)
                    for t in range(tiles):
                        ins = dve.bn_aggr(moments[0:NT, which, t, :], stats[0:NT, which, t, :])
                    ins.then_inc(moments_ready, 1)

                def invert(which):
                    dve.wait_ge(sqrt_done, 2 * n + which + 1)
                    did(dve.reciprocal(rstd[0:NT, which, 0:tiles], stdev[0:NT, which, 0:tiles]))

                def first():
                    did(dve.tensor_scalar(inverse, count, 1.0, None, ALU.max))
                    wait()
                    did(dve.reciprocal(inverse, inverse))
                    wait()
                    did(dve.tensor_tensor(mean, total, inverse, ALU.mult))

                def second(landed, landed_at):
                    dve.wait_ge(landed, landed_at)
                    did(dve.tensor_tensor(xb, x_t, each_row(beta_b), ALU.add))
                    dve.wait_ge(h_ready, n + 1)
                    did(dve.tensor_tensor(r, h, each_row(bias_upd), ALU.add))
                    moments_of(0)

                def third():
                    invert(0)
                    for t in range(tiles):
                        ins = dve.scalar_tensor_tensor(r[:, t, :], r[:, t, :], moments[0:NT, 0, t, 0:1], gamma_b[0:NT, :],
                                                       ALU.subtract, ALU.mult)
                    did(ins)
                    wait()
                    for t in range(tiles):
                        ins = dve.scalar_tensor_tensor(r[:, t, :], r[:, t, :], rstd[0:NT, 0, t:t + 1], xb[:, t, :],
                                                       ALU.mult, ALU.add)
                    did(ins)
                    wait()
                    did(dve.scalar_tensor_tensor(r, r, 0.0, x_t, ALU.max, ALU.add))
                    moments_of(1)

                def fourth(stored=None, stored_at=0):
                    invert(1)
                    wait()
                    if stored is not None:
                        dve.wait_ge(stored, stored_at)
                    for t in range(tiles):
                        ins = dve.tensor_scalar(done[:, t, :], r[:, t, :], moments[0:NT, 1, t, 0:1],
                                                rstd[0:NT, 1, t:t + 1], ALU.subtract, ALU.mult)
                    did(ins)
                    assert at[0] == STEPS, at[0]

                return first, second, third, fourth

            def update_tile(n, t, slot, stats_sems, stats_at):
                return update_steps(n, t, 1, slot, x_buf[:, slot, :, :], xbeta, hid, out_buf[:, slot, :, :],
                                    meanT[:, :], inv[:, :], stats_sems, stats_at)

            def run_block(i, half, early=False, updates=True, stores=True, copies=True, final=False):
                b = block_of(i, half)
                if updates:
                    first, second, third, fourth = update_tile(b - LAG, b - LAG, half,
                                                               stats_ready[2 * half:2 * half + 2], i)
                for s in range(GROUPS):
                    group = GROUPS * b + s
                    slot = GROUPS * half + s
                    make_onehot(i, half, s)
                    if s == 1 and updates:
                        dve.wait_ge(acc_done, GROUPS * b)
                        first()
                    dve.wait_ge(z_ready, group + 1)
                    if not early:
                        blocks_before = i - 2 + half
                        tiles = tiles_with_edges(group) if final else GROUP
                        dve.wait_ge(gathered[slot], 16 * (GROUP * blocks_before + tiles))
                    if early:
                        early_messages(slot, s)
                    else:
                        dve.tensor_tensor(msg[:, s, :], zp[:, s, :], rows[:, slot, :], ALU.add).then_inc(added[slot], 1)
                    if copies:
                        tiles = slice(GROUP * s, GROUP * (s + 1))
                        dve.tensor_copy(gather_idx[:, half, tiles], src_idx[:, b + 2, tiles]).then_inc(idx_ready[slot], 1)
                    if s == 1 and updates:
                        dve.wait_ge(upd_step, STEPS * (b - LAG) + 3)
                    accumulate(group - 1, (s - 1) % GROUPS, base_of(b, s - 1) if s else base_of(b - 1, GROUPS - 1))
                    if s == 2 and updates:
                        if early:
                            dve.wait_ge(consts_in, 16 * 4)
                        second(node_in[half], 32 * i)
                    if s == 3 and updates:
                        third()
                        if final and half == 1:
                            accumulate(group, s % GROUPS, base_of(b, s))
                        if not stores:
                            fourth()
                        else:
                            fourth(out_stored[half], 16 * (i - 1))

            for s in range(GROUPS):
                make_onehot(0, 0, s, first=True)
            for k in range(YRING):
                dve.wait_ge(y_stored[k], 16 * (YGROUPS // YRING))
                dve.memset(y_out[:, k, :], 0.0).then_inc(y_out_zeroed, 1)
            for s in range(GROUPS - 1):
                accumulate(s, s, base_of(0, s), first=(s == 0))
            run_block(0, 1, early=True, updates=False, copies=False)
            run_block(1, 0, early=True, stores=False, copies=False)
            run_block(1, 1, stores=False, copies=False)
            dve.wait_ge(src_in, 16)
            dve.wait_ge(dst_in, 16)
            relative(FIRST, NB).then_inc(dst_rel_made, 1)
            dve.wait_ge(dst_rel_made, 1)
            with dve.Fori(2, NB // 2 - 1) as i:
                run_block(i, 0)
                run_block(i, 1)
            run_block(NB // 2 - 1, 0, copies=False, final=True)
            run_block(NB // 2 - 1, 1, copies=False, final=True)
            dve.wait_ge(acc_done, NS)
            first, second, third, fourth = update_steps(
                UPDATES - 1, NB - LAG, REST, 0, x_last, xbeta_last, hid_last, hid_last, mean_last, inv_last,
                last_stats, 1)
            first()
            second(last_in, 32)
            third()
            fourth()

            broken = dve.value_load(violation[0:1, 0:1], min_val=0, max_val=1)
            with dve.If(broken != 0):
                dve.nop().then_inc(g_added, 1)
                dve.nop().then_inc(g_acc, 1)
                dve.wait_ge(upd_step, STEPS * UPDATES)
                dve.wait_ge(last_stored, 16)
                dve.memset(acc[:, :, :], 0.0).then_inc(g_start, 1)
                dve.wait_ge(g_start, 1)
                with dve.Fori(0, NB) as b:
                    dve.tensor_copy(gather_idx[:, 0, :], src_idx[:, b, :]).then_inc(g_idx, 1)
                    for s in range(GROUPS):
                        dve.wait_ge(g_z, GROUPS * b + s + 2)
                        dve.wait_ge(g_gathered, 16 * TILES * (b + 1))
                        dve.wait_ge(g_used, NWIDE * GROUPS * b + 1)
                        dve.tensor_tensor(msg[:, s, :], zp[:, s, :], rows[:, s, :], ALU.add).then_inc(g_added, 1)
                    dve.tensor_copy(wide_dst[:, :], dst_idx[:, b, :]).then_inc(g_dst, 1)
                    with dve.Fori(0, NWIDE) as w:
                        dve.wait_ge(g_dst, b * (NWIDE + 1) + w + 1)
                        for s in range(GROUPS):
                            dve.wait_ge(g_used, (b * NWIDE + w) * GROUPS + s + 1)
                            dve.tensor_tensor(wide_onehot,
                                              iota_f[:, :].unsqueeze(1).to_broadcast([P, GROUP, WIDE]),
                                              wide_dst[:, GROUP * s:GROUP * (s + 1)].unsqueeze(2)
                                              .to_broadcast([P, GROUP, WIDE]), ALU.is_equal).then_inc(g_onehot, 1)
                        dve.wait_ge(g_onehot, (b * NWIDE + w) * GROUPS + GROUPS)
                        dve.tensor_scalar(wide_dst[:, :], wide_dst[:, :], float(WIDE), None, ALU.subtract)\
                            .then_inc(g_dst, 1)
                        dve.wait_ge(g_used, (b * NWIDE + w) * GROUPS + GROUPS + 1)
                        dve.wait_ge(g_acc, b * NWIDE + w + 1)
                        dve.tensor_tensor(acc[:, :, bass.ds(w * WIDE, WIDE)], acc[:, :, bass.ds(w * WIDE, WIDE)],
                                          sums[:, :, :], ALU.add).then_inc(g_acc, 1)
                dve.wait_ge(g_acc, NB * NWIDE + 1)
                with dve.Fori(1, NTILES + 1) as m:
                    t = m - 1
                    first, second, third, fourth = update_tile(t + UPDATES, t, 0, g_stats, m)
                    first()
                    second(g_node_in, 32 * m)
                    third()
                    fourth(g_stored, 16 * t + 16)
            with dve.Else():
                dve.nop()


def kernel(x, src, dst, edge_attr_128, L0_gnn_W_msg, L0_gnn_b_msg, L0_gnn_W_upd, L0_gnn_b_upd, L0_gnn_gamma,
           L0_gnn_beta):
    import numpy as np
    import concourse.bacc as bacc
    from concourse.bass_utils import run_bass_kernel_spmd

    x, src, dst, edges = (np.asarray(a) for a in (x, src, dst, edge_attr_128))
    n, f = x.shape
    e = src.shape[0]
    NB, NT, NTILES, COLS, _ = sizes(n, e)

    xT = np.zeros((f, COLS), x.dtype)
    xT[:, :n] = x.T
    x_rows = np.zeros((NTILES * NT, f), x.dtype)
    x_rows[:n] = x
    edges_p = np.zeros((NB * BLOCK, f), edges.dtype)
    edges_p[:e] = edges
    src_p = np.zeros((NB * BLOCK,), src.dtype)
    src_p[:e] = src
    dst_p = np.full((NB * BLOCK,), n, dst.dtype)
    dst_p[:e] = dst
    arrays = {
        "xT": xT,
        "x_rows": x_rows,
        "edgesT": np.ascontiguousarray(edges_p.reshape(NB, BLOCK, f).transpose(0, 2, 1)),
        "src_tiles": np.ascontiguousarray(src_p.reshape(NB, TILES, P).transpose(2, 0, 1)),
        "dst_tiles": np.ascontiguousarray(dst_p.reshape(NB, TILES, P).transpose(2, 0, 1)),
        "dst_rows": dst_p.reshape(NB, BLOCK),
        "w_msg": np.asarray(L0_gnn_W_msg),
        "b_msg": np.asarray(L0_gnn_b_msg),
        "w_upd": np.asarray(L0_gnn_W_upd),
        "b_upd": np.asarray(L0_gnn_b_upd),
        "gamma": np.asarray(L0_gnn_gamma),
        "beta": np.asarray(L0_gnn_beta),
    }
    nc = bacc.Bacc("TRN2", target_bir_lowering=False, num_devices=1)
    args = [nc.dram_tensor(name, a.shape, mybir.dt.from_np(a.dtype), kind="ExternalInput").ap()
            for name, a in arrays.items()]
    out = nc.dram_tensor("out", (NTILES * NT, f), mybir.dt.float32, kind="ExternalOutput").ap()
    graph_layer(nc, *args, out, n, e)
    r = run_bass_kernel_spmd(nc, [arrays], core_ids=[0])
    return r.results[0]["out"][:n]
```
